# Optimizing a Trainium2 kernel written in Bass

```python
import numpy as np
import jax
import jax.numpy as jnp

def _softmax(x, axis=-1):
    return jax.nn.softmax(x, axis=axis)

def _gelu(x):
    return jax.nn.gelu(x, approximate=True)

def _silu(x):
    return jax.nn.silu(x)

def _sigmoid(x):
    return jax.nn.sigmoid(x)

def _layernorm(x, axis=-1, eps=1e-05):
    m = jnp.mean(x, axis=axis, keepdims=True)
    v = jnp.var(x, axis=axis, keepdims=True)
    return (x - m) / jnp.sqrt(v + eps)

def _scatter_add(tgt, idx, src, axis=0):
    return tgt.at[idx].add(src)

def _segment_sum(src, seg, n):
    return jax.ops.segment_sum(src, seg, n)
kernel_name = 'mk_lm_tower_d1_tok_ids768_r4_01feb7'

def setup_inputs(seed: int=0):
    np.random.seed(seed)
    _w = jnp.asarray

    def _rec_inputs():
        import jax
        import jax.numpy as jnp
        _rk = jax.random.key(seed)
        x = jax.random.randint(jax.random.fold_in(_rk, 1), (8, 1024), 0, 12564, jnp.int32)
        return x
    x = _rec_inputs()

    def _L0_tok_setup():
        import jax, jax.numpy as jnp
        import numpy as np
        NUM_EMBEDDINGS = 50257
        EMBEDDING_DIM = 192
        key = jax.random.key(seed)
        k_w, k_i = jax.random.split(key)
        weight = jax.random.normal(k_w, (NUM_EMBEDDINGS, EMBEDDING_DIM), dtype=jnp.float32)
        input = jax.random.randint(k_i, (8, 512), 0, NUM_EMBEDDINGS, dtype=jnp.int64)
        return {'input': input, 'weight': weight}
    _L0_tok_all = _L0_tok_setup()
    _L0_tok_in = {k: v for k, v in _L0_tok_all.items() if k in ('weight',)}
    del _L0_tok_all

    def _L0_attn_setup():
        import jax, jax.numpy as jnp
        import numpy as np
        B, S, D, H = (2, 512, 192, 12)
        DK = D // H

        def _split_heads(t):
            b, s, _ = t.shape
            return t.reshape(b, s, H, DK).transpose(0, 2, 1, 3)
        key = jax.random.key(seed)
        ks = jax.random.split(key, 5)
        sigma = (2.0 / (D + D)) ** 0.5

        def w(k):
            return jnp.clip(jax.random.normal(k, (D, D), dtype=jnp.float32) * sigma, -3 * sigma, 3 * sigma)
        return {'x': jax.random.normal(ks[0], (B, S, D), dtype=jnp.float32), 'Wq': w(ks[1]), 'Wk': w(ks[2]), 'Wv': w(ks[3]), 'Wo': w(ks[4])}
    _L0_attn_all = _L0_attn_setup()
    _L0_attn_in = {k: v for k, v in _L0_attn_all.items() if k in ('Wq', 'Wk', 'Wv', 'Wo')}
    del _L0_attn_all

    def _L0_ffn_setup():
        import jax, jax.numpy as jnp
        import numpy as np
        N_HEAD = 8 * 0 + 12
        TOP_K = 2
        GELU_C = 0.7978845608028654

        def _gelu(x):
            return 0.5 * x * (1.0 + jnp.tanh(GELU_C * (x + 0.044715 * x * x * x)))

        def _layernorm_global(x, w, b, eps=1e-12):
            m = jnp.mean(x)
            v = jnp.var(x, ddof=1)
            return (x - m) / jnp.sqrt(v + eps) * w + b

        def _attn(x, W1_w, W1_b, W2_w, W2_b):
            B, N, D = x.shape
            h = N_HEAD
            dh = D // h
            qkv = x @ W1_w + W1_b
            Q, K, V = jnp.split(qkv, 3, axis=-1)
            q = Q.reshape(B, N, h, dh).transpose(0, 2, 3, 1)
            k = K.reshape(B, N, h, dh).transpose(0, 2, 1, 3)
            v = V.reshape(B, N, h, dh).transpose(0, 2, 3, 1)
            w = jax.nn.softmax(q @ k / jnp.sqrt(jnp.asarray(N, x.dtype)), axis=-1)
            out = (w @ v).reshape(B, N, h * dh)
            return out @ W2_w + W2_b

        def _moe(x, r_w, r_b, fc_w, fc_b, proj_w, proj_b):
            B, N, D = x.shape
            scores = x @ r_w + r_b
            gate = jax.nn.softmax(jnp.mean(scores, axis=1), axis=-1)
            vals, idx = jax.lax.top_k(gate, TOP_K)
            hmid = _gelu(jnp.einsum('bnd,edf->benf', x, fc_w) + fc_b[None, :, None, :])
            outs = jnp.einsum('benf,efd->bend', hmid, proj_w) + proj_b[None, :, None, :]
            k_outs = jnp.take_along_axis(outs, idx[:, :, None, None], axis=1)
            return jnp.sum(vals[:, :, None, None] * k_outs, axis=1)
        key = jax.random.key(seed)
        ks = jax.random.split(key, 16)
        B, N, D, E = (2, 512, 192, 8)
        H = 4 * D
        s = 0.02
        return {'x': jax.random.normal(ks[0], (B, N, D), jnp.float32), 'W1_w': jax.random.normal(ks[1], (D, 3 * D), jnp.float32) * s, 'W1_b': jnp.zeros((3 * D,), jnp.float32), 'W2_w': jax.random.normal(ks[2], (D, D), jnp.float32) * s, 'W2_b': jnp.zeros((D,), jnp.float32), 'r_w': jax.random.normal(ks[3], (D, E), jnp.float32) * s, 'r_b': jnp.zeros((E,), jnp.float32), 'fc_w': jax.random.normal(ks[4], (E, D, H), jnp.float32) * s, 'fc_b': jnp.zeros((E, H), jnp.float32), 'proj_w': jax.random.normal(ks[5], (E, H, D), jnp.float32) * s, 'proj_b': jnp.zeros((E, D), jnp.float32), 'ln1_w': jnp.ones((D,), jnp.float32), 'ln1_b': jnp.zeros((D,), jnp.float32), 'ln2_w': jnp.ones((D,), jnp.float32), 'ln2_b': jnp.zeros((D,), jnp.float32)}
    _L0_ffn_all = _L0_ffn_setup()
    _L0_ffn_in = {k: v for k, v in _L0_ffn_all.items() if k in ('W1_w', 'W1_b', 'W2_w', 'W2_b', 'r_w', 'r_b', 'fc_w', 'fc_b', 'proj_w', 'proj_b', 'ln1_w', 'ln1_b', 'ln2_w', 'ln2_b')}
    del _L0_ffn_all
    return {'x': x, 'L0_tok_weight': _L0_tok_in['weight'], 'L0_attn_Wq': _L0_attn_in['Wq'], 'L0_attn_Wk': _L0_attn_in['Wk'], 'L0_attn_Wv': _L0_attn_in['Wv'], 'L0_attn_Wo': _L0_attn_in['Wo'], 'L0_ffn_W1_w': _L0_ffn_in['W1_w'], 'L0_ffn_W1_b': _L0_ffn_in['W1_b'], 'L0_ffn_W2_w': _L0_ffn_in['W2_w'], 'L0_ffn_W2_b': _L0_ffn_in['W2_b'], 'L0_ffn_r_w': _L0_ffn_in['r_w'], 'L0_ffn_r_b': _L0_ffn_in['r_b'], 'L0_ffn_fc_w': _L0_ffn_in['fc_w'], 'L0_ffn_fc_b': _L0_ffn_in['fc_b'], 'L0_ffn_proj_w': _L0_ffn_in['proj_w'], 'L0_ffn_proj_b': _L0_ffn_in['proj_b'], 'L0_ffn_ln1_w': _L0_ffn_in['ln1_w'], 'L0_ffn_ln1_b': _L0_ffn_in['ln1_b'], 'L0_ffn_ln2_w': _L0_ffn_in['ln2_w'], 'L0_ffn_ln2_b': _L0_ffn_in['ln2_b']}

def reference(x, L0_tok_weight, L0_attn_Wq, L0_attn_Wk, L0_attn_Wv, L0_attn_Wo, L0_ffn_W1_w, L0_ffn_W1_b, L0_ffn_W2_w, L0_ffn_W2_b, L0_ffn_r_w, L0_ffn_r_b, L0_ffn_fc_w, L0_ffn_fc_b, L0_ffn_proj_w, L0_ffn_proj_b, L0_ffn_ln1_w, L0_ffn_ln1_b, L0_ffn_ln2_w, L0_ffn_ln2_b):
    import jax
    import jax.numpy as jnp

    def _L0_tok_ref(input, weight):
        import jax, jax.numpy as jnp
        import numpy as np
        NUM_EMBEDDINGS = 50257
        EMBEDDING_DIM = 192
        return jnp.take(weight, input, axis=0)

    def _L0_attn_ref(x, Wq, Wk, Wv, Wo):
        import jax, jax.numpy as jnp
        import numpy as np
        B, S, D, H = (2, 512, 192, 12)
        DK = D // H

        def _split_heads(t):
            b, s, _ = t.shape
            return t.reshape(b, s, H, DK).transpose(0, 2, 1, 3)
        q = _split_heads(jnp.einsum('bsd,od->bso', x, Wq))
        k = _split_heads(jnp.einsum('bsd,od->bso', x, Wk))
        v = _split_heads(jnp.einsum('bsd,od->bso', x, Wv))
        norm = jax.lax.rsqrt(jnp.asarray(DK, dtype=x.dtype))
        scores = jnp.einsum('bhid,bhjd->bhij', q, k) * norm
        s = x.shape[-2]
        causal = jnp.tril(jnp.ones((s, s), dtype=bool))
        scores = jnp.where(causal, scores, -jnp.inf)
        attn = jax.nn.softmax(scores, axis=-1)
        out = jnp.einsum('bhij,bhjd->bhid', attn, v)
        out = out.transpose(0, 2, 1, 3).reshape(x.shape[0], s, D)
        return jnp.einsum('bsd,od->bso', out, Wo)

    def _L0_ffn_ref(x, W1_w, W1_b, W2_w, W2_b, r_w, r_b, fc_w, fc_b, proj_w, proj_b, ln1_w, ln1_b, ln2_w, ln2_b):
        import jax, jax.numpy as jnp
        import numpy as np
        N_HEAD = 8 * 0 + 12
        TOP_K = 2
        GELU_C = 0.7978845608028654

        def _gelu(x):
            return 0.5 * x * (1.0 + jnp.tanh(GELU_C * (x + 0.044715 * x * x * x)))

        def _layernorm_global(x, w, b, eps=1e-12):
            m = jnp.mean(x)
            v = jnp.var(x, ddof=1)
            return (x - m) / jnp.sqrt(v + eps) * w + b

        def _attn(x, W1_w, W1_b, W2_w, W2_b):
            B, N, D = x.shape
            h = N_HEAD
            dh = D // h
            qkv = x @ W1_w + W1_b
            Q, K, V = jnp.split(qkv, 3, axis=-1)
            q = Q.reshape(B, N, h, dh).transpose(0, 2, 3, 1)
            k = K.reshape(B, N, h, dh).transpose(0, 2, 1, 3)
            v = V.reshape(B, N, h, dh).transpose(0, 2, 3, 1)
            w = jax.nn.softmax(q @ k / jnp.sqrt(jnp.asarray(N, x.dtype)), axis=-1)
            out = (w @ v).reshape(B, N, h * dh)
            return out @ W2_w + W2_b

        def _moe(x, r_w, r_b, fc_w, fc_b, proj_w, proj_b):
            B, N, D = x.shape
            scores = x @ r_w + r_b
            gate = jax.nn.softmax(jnp.mean(scores, axis=1), axis=-1)
            vals, idx = jax.lax.top_k(gate, TOP_K)
            hmid = _gelu(jnp.einsum('bnd,edf->benf', x, fc_w) + fc_b[None, :, None, :])
            outs = jnp.einsum('benf,efd->bend', hmid, proj_w) + proj_b[None, :, None, :]
            k_outs = jnp.take_along_axis(outs, idx[:, :, None, None], axis=1)
            return jnp.sum(vals[:, :, None, None] * k_outs, axis=1)
        a = _attn(x, W1_w, W1_b, W2_w, W2_b)
        x = _layernorm_global(a + x, ln1_w, ln1_b)
        m = _moe(x, r_w, r_b, fc_w, fc_b, proj_w, proj_b)
        x = _layernorm_global(m + x, ln2_w, ln2_b)
        return x
    h = _L0_tok_ref(x, L0_tok_weight)
    h = h + _L0_attn_ref(_layernorm(h, axis=-1), L0_attn_Wq, L0_attn_Wk, L0_attn_Wv, L0_attn_Wo)
    h = h + _L0_ffn_ref(_layernorm(h, axis=-1), L0_ffn_W1_w, L0_ffn_W1_b, L0_ffn_W2_w, L0_ffn_W2_b, L0_ffn_r_w, L0_ffn_r_b, L0_ffn_fc_w, L0_ffn_fc_b, L0_ffn_proj_w, L0_ffn_proj_b, L0_ffn_ln1_w, L0_ffn_ln1_b, L0_ffn_ln2_w, L0_ffn_ln2_b)
    return h

_drawn_inputs = setup_inputs


def setup_inputs(seed=0):
    import zlib

    import numpy as np

    out = dict(_drawn_inputs(seed))
    spreads = {'L0_ffn_W1_b': (0.0, 0.8),
     'L0_ffn_W2_b': (0.0, 0.1),
     'L0_ffn_r_b': (0.0, 0.44),
     'L0_ffn_fc_b': (0.0, 0.8),
     'L0_ffn_proj_b': (0.0, 0.8),
     'L0_ffn_ln1_w': (1.0, 0.2),
     'L0_ffn_ln1_b': (0.0, 0.1),
     'L0_ffn_ln2_w': (1.0, 0.2),
     'L0_ffn_ln2_b': (0.0, 0.1)}
    factors = {'L0_ffn_W1_w': 5.266,
     'L0_ffn_W2_w': 5.209,
     'L0_ffn_r_w': 8.0,
     'L0_ffn_fc_w': 6.643,
     'L0_ffn_proj_w': 6.147}
    for name, (base, spread) in spreads.items():
        noise = np.random.default_rng([zlib.crc32(name.encode()), seed]).standard_normal(out[name].shape)
        drawn = base * np.exp(spread * noise) if base else spread * noise
        out[name] = jnp.asarray(drawn.astype(out[name].dtype))
    for name, factor in factors.items():
        out[name] = (out[name] * factor).astype(out[name].dtype)
    return out
```

```python
import concourse.bass as bass
from concourse import mybir
from contextlib import ExitStack

B, N, D = 8, 1024, 192
HEADS, DH = 12, 16
P = 128
GROUP = 4
G = HEADS // GROUP
TT = N // P
HALF = 512
NH = N // HALF
KD = 96
KT = D // KD
SLOTS = 6
STACK = SLOTS * DH
SHIFT = 2
VW = DH + 1
E, F = 8, 768
FT = F // P
TOP = 2
NEG = -1.0e30
LOWEST = -3.0e38
LN_EPS, GLOBAL_EPS = 1e-5, 1e-12
SCORE_SCALE, CHANNEL_SCALE = DH ** -0.5, N ** -0.5
Q_PARTS = (0, 0, 1, 1, 0, 2)
K_PARTS = (0, 1, 0, 1, 2, 0)
TALL = (KD, KD + 1)
RUN = KD
MOMENTS, VARIANCE = 1, 6
YSUM, XMEAN, NEGTOP, CHOSEN, GATES = 13, 15, 17, 21, 22
MOMENTS_2, VARIANCE_2, ADDEND = 23, 28, 31



def key_tiles(half):
    return range(4 * (half + 1))


def diagonal(half, kt):
    return kt // 4 == half


def first_column(half, kt):
    return max(0, P * kt - HALF * half)


def max_tiles(half):
    return [(t, h, c) for t in range(4 * half, 4 * half + 4) for h in range(GROUP) for c in range(t // 4 + 1)]


class Order:

    BANKED = {"QK": "prep", "V": "prep", "XT": "prep", "SHIFT": "side", "SUMS": "side", "NORM": "side", "OUT": "side"}

    def __init__(self):
        self.jobs, self.count = [], {}

    def add(self, kind, **what):
        self.jobs.append((kind, what | {"before": dict(self.count)}))
        self.tally(kind)
        if kind in self.BANKED:
            self.tally(self.BANKED[kind])

    def tally(self, kind):
        self.count[kind] = self.count.get(kind, 0) + 1


def max_jobs(o, g, half, ahead):
    for t, h, c in max_tiles(half):
        yield lambda t=t, h=h, c=c: o.add("MAX", g=g, t=t, h=h, c=c, ahead=ahead)
    yield lambda: o.add("NEGATE", g=g, half=half)


def step(o, g, maxi, prep, next_ln):
    for half in range(NH):
        side = []
        if half == 0:
            if g > 0:
                side += [("SUMS", dict(g=g - 1, half=1)), ("NORM", dict(g=g - 1, half=1))]
            side.append(("SHIFT", dict(g=g, half=1)))
            if prep is not None:
                side += [("QK", dict(g=prep, half=i)) for i in range(NH)]
                side += [("STACK", dict(g=prep)), ("V", dict(g=prep))]
            if next_ln:
                side.append(("LN", {}))
        else:
            side += [("SUMS", dict(g=g, half=0)), ("NORM", dict(g=g, half=0))]
            if maxi is not None:
                side.append(("SHIFT", dict(g=maxi, half=0)))
            if next_ln:
                side += [("XT", dict(k=k, half=i)) for k in range(KT) for i in range(NH)]
            if g == G - 1:
                side += [("OUT", dict(pair=i)) for i in range(2)]
        kts = list(key_tiles(half))
        maxima = list(max_jobs(o, maxi, half, 1)) if maxi is not None else []
        per = -(-len(maxima) // (GROUP * len(kts)))
        for i in range(len(kts) + 1):
            if i < len(kts):
                for h in range(GROUP):
                    o.add("SCORE", g=g, half=half, kt=kts[i], h=h)
                    for _ in range(min(per, len(maxima))):
                        maxima.pop(0)()
                o.tally("BLOCK")
            else:
                while maxima:
                    maxima.pop(0)()
            if i > 0:
                o.add("VALUE", g=g, half=half, kt=kts[i - 1], last=i == len(kts))
                if diagonal(half, kts[i - 1]):
                    o.tally("DIAGONAL")
                for _ in range(-(-len(side) // (len(kts) + 1 - i))):
                    kind, what = side.pop(0)
                    o.add(kind, **what)
        o.add("EVAC", g=g, half=half)
    if g == G - 1:
        o.add("SUMS", g=g, half=1)
        o.add("NORM", g=g, half=1)
        for i in range(2, 4):
            o.add("OUT", pair=i)
    o.tally("UNIT")


def head_order():
    o = Order()
    o.add("LN")
    for k in range(KT):
        for i in range(NH):
            o.add("XT", k=k, half=i)
    for g in range(2):
        for i in range(NH):
            o.add("QK", g=g, half=i)
        o.add("STACK", g=g)
        o.add("V", g=g)
    for half in range(NH):
        for job in max_jobs(o, 0, half, 0):
            job()
    o.add("SHIFT", g=0, half=0)
    return o


def batch_order(last):
    o = Order()
    units = list(range(G)) + [None if last else g for g in range(G - 1)]
    for g in range(G):
        step(o, units[g], units[g + 1], units[g + 2], g == 0 and not last)
    return o


def channel_head():
    o = Order()
    o.add("LN")
    for i in range(KT):
        o.add("GRAM", i=i)
    for i in range(4):
        o.add("XT", k=i // NH, half=i % NH)
    o.add("LN")
    return o


def channel_order(gram, norm):
    o = Order()
    o.add("MIX")
    if gram:
        o.add("GRAM", i=0)
    o.add("SCORES")
    if gram:
        o.add("GRAM", i=1)
    o.add("TURN")
    o.add("UNITE")
    for i in range(4):
        o.add("ROWS", a=i // 2, half=i % 2)
    if gram:
        for i in range(4):
            o.add("XT", k=i // NH, half=i % NH)
    for i in range(4):
        o.add("OUT", pair=i)
    if norm:
        o.add("LN")
    return o


def stretches(head, parts):
    out, start, first = [], dict(head.count), 0
    for order, times in parts:
        out.append((times if times > 1 else None, first, order, dict(start)))
        first += times
        for kind, n in order.count.items():
            start[kind] = start.get(kind, 0) + n * times
    return out


class Numbers:

    def __init__(self, start, per, loop, eng=None):
        self.start, self.per, self.loop, self.eng, self.held = start, per, loop, eng, {}

    def __call__(self, kind, what, each=1, more=0):
        fixed = each * (self.start.get(kind, 0) + what["before"].get(kind, 0)) + more
        per = each * self.per.get(kind, 0)
        if not per or isinstance(self.loop, int):
            return fixed
        if per not in self.held:
            self.held[per] = self.eng.snap(self.loop * per)
        return self.held[per] + fixed


def pieces(flat):
    out, at = [], 0
    while at < RUN:
        r, token = divmod(flat + at, N)
        count = min(RUN - at, N - token)
        if at % 64 and count > 32:
            count = 32
        out.append((at, count, r, token))
        at += count
    return out


def build(nc, tok, table, wqk, wv, wo, wk2, wq2, wvT2, w2, r_w, r_b, fc_w, fc_b, pj_w, pj_b, ln, ln_cols, out):
    f32, bf16, i32, u32 = mybir.dt.float32, mybir.dt.bfloat16, mybir.dt.int32, mybir.dt.uint32
    ALU, ACT, AX = mybir.AluOpType, mybir.ActivationFunctionType, mybir.AxisListType
    nc.disable_value_cache = True
    HEAD = head_order()
    STRETCHES = stretches(HEAD, [(batch_order(False), B - 1), (batch_order(True), 1)])
    HEAD_2 = channel_head()
    STRETCHES_2 = stretches(HEAD_2, [(channel_order(True, True), B - 2), (channel_order(True, False), 1),
                                     (channel_order(False, False), 1)])

    whole = ExitStack()
    with whole:
        def keep(name, shape, dt):
            return whole.enter_context(nc.sbuf_tensor(name, shape, dt))
        hid = keep("hid", [P, B * TT, D], f32)
        ident = keep("ident", [P, P], f32)
        minus_half = keep("minus_half", [P, TT], f32)
        stat = keep("stat", [P, TT, nc.vector.BN_STATS_DIM], f32)
        mean_var = keep("mean_var", [P, TT, 2], f32)
        rstd = keep("rstd", [P, TT], f32)

        def run_stretches(eng, work, head, parts):
            work(head, Numbers({}, {}, 0), 0)
            for batches, first, order, start in parts:
                if batches:
                    with eng.Fori(0, batches) as b:
                        work(order, Numbers(start, order.count, b, eng), b)
                else:
                    work(order, Numbers(start, {}, 0), first)

        def wait(eng, sem, value):
            if not isinstance(value, int) or value > 0:
                eng.wait_ge(sem, value)

        attn = ExitStack()
        with attn:
            def sb(name, shape, dt):
                return attn.enter_context(nc.sbuf_tensor(name, shape, dt))

            def pb(name, shape, dt=f32):
                return attn.enter_context(nc.psum_tensor(name, shape, dt))

            def sem(name):
                return attn.enter_context(nc.semaphore(name))

            ids = sb("ids", [P, B * TT], i32)
            wqk_sb = sb("wqk_sb", [KD, G, KT, P], f32)
            wv_sb = sb("wv_sb", [KD, KT, D], f32)
            wo_sb = sb("wo_sb", [P, G, D], f32)
            xT = sb("xT", [KD, KT, N], f32)
            part = [sb(f"part{i}", [P, N], bf16) for i in range(3)]
            rest = sb("rest", [P, HALF], f32)
            qs = sb("qs", [STACK + SHIFT, G, GROUP, N], bf16)
            ks = sb("ks", [STACK + SHIFT, G, GROUP, N], bf16)
            v = sb("v", [P, G, TT, GROUP, VW], f32)
            prob = sb("prob", [P, 2, GROUP, HALF], f32)
            maxima = sb("maxima", [P, TT, GROUP, NH], f32)
            negmax = sb("negmax", [P, TT, GROUP], f32)
            negpart = sb("negpart", [P, TT, SHIFT, GROUP], bf16)
            shift_row = sb("shift_row", [SHIFT * GROUP, HALF], bf16)
            mask = sb("mask", [P, HALF], bf16)
            identb = sb("identb", [P, P], bf16)
            pick = sb("pick", [P, GROUP], f32)
            rsum = sb("rsum", [P, 4 * GROUP], f32)
            rsum_b = sb("rsum_b", [P, 4, GROUP, 32], f32)
            on = sb("on", [P, G, N], f32)

            fresh = on[:, 1:G, :].rearrange("p g n -> p (g n)")[:, 0:TT * D].rearrange("p (t d) -> p t d", d=D)

            max_ps = pb("max_ps", [P, 2, HALF])
            score_ps = pb("score_ps", [P, 2, HALF])
            o_ps = pb("o_ps", [P, NH, HALF])
            prep_ps = pb("prep_ps", [P, HALF])
            side_ps = pb("side_ps", [P, HALF])
            side_ps16 = side_ps[:, :].bitcast(bf16)

            ids_in = sem("ids_in")
            weights_in = sem("weights_in")
            gathered = [sem(f"gathered{b}") for b in range(B)]
            landed = sem("landed")
            const_pool = sem("const_pool")
            const_dve = sem("const_dve")
            stats_done = sem("stats_done")
            rstd_done = sem("rstd_done")
            ln_done = sem("ln_done")
            prep_filled = sem("prep_filled")
            prep_drained = sem("prep_drained")
            part1_done = sem("part1_done")
            part2_done = sem("part2_done")
            part3_done = sem("part3_done")
            stacked = sem("stacked")
            max_filled = sem("max_filled")
            max_drained = sem("max_drained")
            negated = sem("negated")
            side_filled = sem("side_filled")
            side_drained = sem("side_drained")
            sums_spread = sem("sums_spread")
            shifted = sem("shifted")
            score_filled = sem("score_filled")
            exp_done = sem("exp_done")
            masked = sem("masked")
            value_done = sem("value_done")
            o_evacuated = sem("o_evacuated")

            STACK_DMAS = 16 * 2 * SLOTS
            SHIFT_DMAS = 16 * SHIFT
            block = attn.enter_context(nc.Block())

            passed = {eng: sem(f"passed_{name}") for name, eng in
                      (("vector", nc.vector), ("gpsimd", nc.gpsimd))}

            def run(eng, work):
                run_stretches(eng, work, HEAD, STRETCHES)

            def apart(eng):
                eng.sem_inc(passed[eng], 1)

            def half_of(w):
                return slice(HALF * w["half"], HALF * (w["half"] + 1))

            @block.sync
            def _(sp):
                sp.dma_start(ids[:, :], tok).then_inc(ids_in, 16)
                for dst, src in ((wqk_sb, wqk), (wv_sb, wv), (wo_sb, wo)):
                    sp.dma_start(dst[:], src).then_inc(weights_in, 16)
                sp.wait_ge(const_dve, 4)

                def work(order, before, b):
                    for kind, w in order.jobs:
                        if kind == "STACK":
                            sp.wait_ge(part3_done, before("QK", w))
                            for s in range(SLOTS):
                                for dst, which, row in ((qs, Q_PARTS[s], 0), (ks, K_PARTS[s], P // 2)):
                                    sp.dma_start(dst[DH * s:DH * (s + 1), w["g"], :, :],
                                                 part[which][row:row + P // 2, :]).then_inc(stacked, 16)
                        if kind == "SHIFT":
                            sp.wait_ge(side_drained, before("side", w, 1, 2))
                            for r in range(SHIFT):
                                sp.dma_start(qs[STACK + r:STACK + r + 1, w["g"], :, half_of(w)],
                                             shift_row[GROUP * r:GROUP * (r + 1), :]).then_inc(shifted, 16)

                run(sp, work)

            @block.gpsimd
            def _(pool):
                pool.memset(ident[:, :], 0.0).then_inc(const_pool, 1)
                pool.memset(identb[:, :], 0.0).then_inc(const_pool, 1)
                pool.memset(pick[:, :], 0.0).then_inc(const_pool, 1)
                pool.memset(mask[:, :], 0.0).then_inc(const_pool, 1)
                pool.memset(minus_half[:, :], -0.5).then_inc(const_pool, 1)
                pool.wait_ge(const_pool, 5)
                for m in (ident, identb):
                    pool.affine_select(out=m[:, :], in_=m[:, :], compare_op=ALU.not_equal, fill=1.0, base=0,
                                       pattern=[[-1, P]], channel_multiplier=1).then_inc(const_pool, 1)
                pool.affine_select(out=pick[:, :], in_=pick[:, :], compare_op=ALU.not_equal, fill=1.0, base=-DH,
                                   pattern=[[-32, GROUP]], channel_multiplier=1).then_inc(const_pool, 1)
                pool.affine_select(out=mask[:, HALF - P:HALF], in_=mask[:, HALF - P:HALF], compare_op=ALU.is_ge,
                                   fill=NEG, base=0, pattern=[[-1, P]], channel_multiplier=1).then_inc(const_pool, 1)
                pool.wait_ge(ids_in, 16)
                for b in range(B):
                    for t in range(TT):
                        i = TT * b + t
                        pool.indirect_dma_start(
                            out=hid[:, i, :], out_offset=None, in_=table,
                            in_offset=bass.IndirectOffsetOnAxis(ap=ids[:, i:i + 1].bitcast(u32), axis=0)
                        ).then_inc(gathered[b], 16)
                for b in range(B):
                    pool.wait_ge(gathered[b], 16 * TT)
                    pool.sem_inc(landed, 1)

                def work(order, before, b):
                    for kind, w in order.jobs:
                        if kind == "LN":
                            pool.wait_ge(stats_done, before("LN", w, 2 * TT, 2 * TT))
                            apart(pool)
                            pool.tensor_scalar(rstd[:, :], mean_var[:, :, 1], LN_EPS, None, ALU.add).then_inc(rstd_done, 1)
                            pool.wait_ge(rstd_done, before("LN", w, 2, 1))
                            pool.tensor_tensor(rstd[:, :], rstd[:, :], minus_half[:, :], ALU.pow).then_inc(rstd_done, 1)
                        if kind == "QK":
                            c = half_of(w)
                            pool.wait_ge(prep_drained, before("prep", w, 1, 2))
                            apart(pool)
                            pool.tensor_copy(part[1][:, c], rest[:, :]).then_inc(part2_done, 1)
                            pool.wait_ge(part2_done, before("QK", w, 1, 1))
                            pool.tensor_tensor(part[2][:, c], rest[:, :], part[1][:, c], ALU.subtract).then_inc(part3_done, 1)
                        if kind == "SUMS":
                            pool.wait_ge(side_drained, before("side", w, 1, 2))
                            apart(pool)
                            pool.tensor_copy(rsum_b[:, :, :, :],
                                             rsum[:, :].rearrange("p (t h) -> p t h", h=GROUP)
                                             .unsqueeze(3).to_broadcast([P, 4, GROUP, 32])).then_inc(sums_spread, 1)
                        if kind == "SCORE" and diagonal(w["half"], w["kt"]) and w["h"] == GROUP - 1:
                            pool.wait_ge(exp_done, before("SCORE", w, 1, 3))
                            c = first_column(w["half"], w["kt"])
                            tile = prob[:, w["before"].get("BLOCK", 0) % 2, :, c:c + P]
                            apart(pool)
                            pool.affine_select(out=tile, in_=tile, compare_op=ALU.is_ge, fill=0.0, base=0,
                                               pattern=[[0, GROUP], [1, P]], channel_multiplier=-1).then_inc(masked, 1)

                run(pool, work)

            @block.scalar
            def _(act):
                act.sem_inc(exp_done, 2)
                act.sem_inc(o_evacuated, NH)
                act.wait_ge(weights_in, 16 * 3)
                act.wait_ge(const_dve, 4)

                def work(order, before, b):
                    for kind, w in order.jobs:
                        if kind == "XT":
                            act.wait_ge(prep_filled, before("prep", w, 1, 1))
                            act.activation(xT[:, w["k"], half_of(w)], prep_ps[0:KD, :], ACT.Copy).then_inc(prep_drained, 1)
                        if kind == "QK":
                            wait(act, stacked, before("STACK", w, STACK_DMAS))
                            act.wait_ge(prep_filled, before("prep", w, 1, 1))
                            act.activation(part[0][:, half_of(w)], prep_ps[:, :], ACT.Copy).then_inc(part1_done, 1)
                        if kind == "SHIFT":
                            wait(act, shifted, before("SHIFT", w, SHIFT_DMAS))
                            act.wait_ge(side_filled, before("side", w, 1, 1))
                            act.activation(shift_row[:, :], side_ps16[0:SHIFT * GROUP, 0:HALF], ACT.Copy).then_inc(side_drained, 1)
                        if kind == "SCORE":
                            c = first_column(w["half"], w["kt"])
                            if w["h"] == 0:
                                act.wait_ge(value_done, before("BLOCK", w, 1, 1))
                            act.wait_ge(score_filled, before("SCORE", w, 1, 1))
                            act.activation(prob[:, w["before"].get("BLOCK", 0) % 2, w["h"], c:HALF],
                                           score_ps[:, w["before"].get("SCORE", 0) % 2, c:HALF],
                                           ACT.Exp, scale=SCORE_SCALE).then_inc(exp_done, 1)
                        if kind == "EVAC":
                            act.wait_ge(side_drained, before("side", w, 1, 1))
                            act.wait_ge(value_done, before("VALUE", w, 1, 2))
                            act.activation(on[:, w["g"], half_of(w)], o_ps[:, w["half"], :], ACT.Copy).then_inc(o_evacuated, 1)

                run(act, work)

            @block.vector
            def _(dve):
                dve.memset(v[:, :, :, :, DH:VW], 1.0).then_inc(const_dve, 1)
                dve.memset(ks[STACK:STACK + SHIFT, :, :, :], 1.0).then_inc(const_dve, 1)
                dve.memset(o_ps[:, :, :], 0.0).then_inc(const_dve, 1)
                dve.memset(maxima[:, :, :, :], LOWEST).then_inc(const_dve, 1)
                dve.sem_inc(max_drained, 2)
                dve.sem_inc(side_drained, 1)
                dve.sem_inc(prep_drained, 1)
                dve.wait_ge(const_dve, 4)
                dve.wait_ge(const_pool, 9)
                dve.wait_ge(weights_in, 16 * 3)

                def row(x, i):
                    return x[:, bass.ds(i, 1), :].rearrange("p a d -> p (a d)")

                def work(order, before, b):
                    for kind, w in order.jobs:
                        if kind == "LN":
                            nb = 0 if order is HEAD else b + 1
                            dve.wait_ge(landed, nb + 1)
                            for t in range(TT):
                                dve.bn_stats(stat[:, t, :], row(hid, TT * nb + t)).then_inc(stats_done, 1)
                            dve.wait_ge(stats_done, before("LN", w, 2 * TT, TT))
                            apart(dve)
                            for t in range(TT):
                                dve.bn_aggr(mean_var[:, t, :], stat[:, t, :]).then_inc(stats_done, 1)
                            dve.wait_ge(rstd_done, before("LN", w, 2, 2))
                            for t in range(TT):
                                dve.tensor_scalar(fresh[:, t, :], row(hid, TT * nb + t), mean_var[:, t, 0:1],
                                                  rstd[:, t:t + 1], ALU.subtract, ALU.mult).then_inc(ln_done, 1)
                        if kind == "QK":
                            dve.wait_ge(part1_done, before("QK", w, 1, 1))
                            wait(dve, part3_done, before("QK", w))
                            dve.tensor_tensor(rest[:, :], prep_ps[:, :], part[0][:, half_of(w)],
                                              ALU.subtract).then_inc(prep_drained, 1)
                        if kind == "V":
                            dve.wait_ge(prep_filled, before("prep", w, 1, 1))
                            dve.tensor_copy(v[:, w["g"], :, :, 0:DH],
                                            prep_ps[:, :].rearrange("p (t h d) -> p t h d", h=GROUP, d=DH)).then_inc(prep_drained, 1)
                        if kind == "MAX":
                            dve.wait_ge(max_filled, before("MAX", w, 1, 1))
                            n = w["before"].get("MAX", 0)
                            to = maxima[:, w["t"], w["h"], w["c"]:w["c"] + 1]
                            if w["c"] == w["t"] // 4:
                                keys = P * (w["t"] % 4 + 1)
                                apart(dve)
                                dve.tensor_tensor_reduce(out=max_ps[:, n % 2, 0:keys], in0=max_ps[:, n % 2, 0:keys],
                                                         in1=mask[:, HALF - keys:HALF], scale=1.0, scalar=LOWEST,
                                                         op0=ALU.add, op1=ALU.max, accum_out=to).then_inc(max_drained, 1)
                            else:
                                dve.tensor_reduce(to, max_ps[:, n % 2, :], AX.X, ALU.max).then_inc(max_drained, 1)
                        if kind == "NEGATE":
                            ts = slice(4 * w["half"], 4 * w["half"] + 4)
                            seen = w["half"] + 1
                            dve.wait_ge(max_drained, before("MAX", w, 1, 2))
                            dve.tensor_reduce(negmax[:, ts, :], maxima[:, ts, :, 0:seen], AX.X, ALU.max,
                                              negate=True).then_inc(negated, 1)
                            dve.wait_ge(negated, before("NEGATE", w, 3, 1))
                            dve.tensor_copy(negpart[:, ts, 0, :], negmax[:, ts, :]).then_inc(negated, 1)
                            dve.wait_ge(negated, before("NEGATE", w, 3, 2))
                            dve.tensor_tensor(negpart[:, ts, 1, :], negmax[:, ts, :], negpart[:, ts, 0, :],
                                              ALU.subtract).then_inc(negated, 1)
                        if kind == "SUMS":
                            dve.wait_ge(side_filled, before("side", w, 1, 1))
                            dve.reciprocal(rsum[:, :], side_ps[:, 0:4 * GROUP]).then_inc(side_drained, 1)
                        if kind == "NORM":
                            dve.wait_ge(side_filled, before("side", w, 1, 1))
                            dve.tensor_tensor(on[:, w["g"], half_of(w)], on[:, w["g"], half_of(w)], side_ps[:, :],
                                              ALU.mult).then_inc(side_drained, 1)
                        if kind == "OUT":
                            dve.wait_ge(side_filled, before("side", w, 1, 1))
                            rows = hid[:, bass.ds(TT * b + 2 * w["pair"], 2), :]
                            dve.tensor_tensor(rows, side_ps[:, 0:2 * D].rearrange("p (t d) -> p t d", d=D), rows,
                                              ALU.add).then_inc(side_drained, 1)

                run(dve, work)

            @block.tensor
            def _(pe):
                pe.sem_inc(value_done, 2)
                pe.wait_ge(const_pool, 9)
                pe.wait_ge(const_dve, 4)
                pe.wait_ge(weights_in, 16 * 3)

                def transpose(out, in_, one):
                    return pe.matmul(out, in_, one, is_transpose=True, start=True, stop=True)

                def work(order, before, b):
                    for kind, w in order.jobs:
                        if kind in ("XT", "QK", "V"):
                            if kind == "XT" and w["k"] == 0 and w["half"] == 0:
                                pe.wait_ge(ln_done, before("LN", w, TT))
                            pe.wait_ge(prep_drained, before("prep", w, 1, 1))
                        if kind in ("SHIFT", "SUMS", "NORM", "OUT"):
                            pe.wait_ge(side_drained, before("side", w, 1, 1))
                        if kind == "XT":
                            for t in range(4):
                                ins = transpose(prep_ps[0:KD, P * t:P * (t + 1)],
                                                fresh[:, 4 * w["half"] + t, KD * w["k"]:KD * (w["k"] + 1)], ident[:, :])
                            ins.then_inc(prep_filled, 1)
                        if kind == "QK":
                            for k in range(KT):
                                ins = pe.matmul(prep_ps[:, :], wqk_sb[:, w["g"], k, :],
                                                xT[:, k, half_of(w)], start=k == 0, stop=k == KT - 1)
                            ins.then_inc(prep_filled, 1)
                        if kind == "V":
                            for t in range(TT):
                                for k in range(KT):
                                    ins = pe.matmul(prep_ps[:, 64 * t:64 * (t + 1)], xT[:, k, P * t:P * (t + 1)],
                                                    wv_sb[:, k, 64 * w["g"]:64 * (w["g"] + 1)],
                                                    start=k == 0, stop=k == KT - 1)
                            ins.then_inc(prep_filled, 1)
                        if kind == "MAX":
                            if w["t"] == 0 and w["h"] == 0 and w["c"] == 0:
                                pe.wait_ge(stacked, before("UNIT", w, STACK_DMAS, STACK_DMAS * (w["ahead"] + 1)))
                            pe.wait_ge(max_drained, before("MAX", w, 1, 1))
                            n = w["before"].get("MAX", 0)
                            keys = P * (w["t"] % 4 + 1) if w["c"] == w["t"] // 4 else HALF
                            pe.matmul(max_ps[:, n % 2, 0:keys], qs[0:STACK, w["g"], w["h"], P * w["t"]:P * (w["t"] + 1)],
                                      ks[0:STACK, w["g"], w["h"], HALF * w["c"]:HALF * w["c"] + keys],
                                      start=True, stop=True).then_inc(max_filled, 1)
                        if kind == "SHIFT":
                            pe.wait_ge(negated, before("SHIFT", w, 3, 3))
                            for t in range(4):
                                ins = transpose(side_ps16[0:SHIFT * GROUP, P * t:P * (t + 1)],
                                                negpart[:, 4 * w["half"] + t, :, :].rearrange("p s h -> p (s h)"), identb[:, :])
                            ins.then_inc(side_filled, 1)
                        if kind == "SCORE":
                            c = first_column(w["half"], w["kt"])
                            if w["kt"] == 0 and w["h"] == 0:
                                pe.wait_ge(shifted, before("UNIT", w, 2 * SHIFT_DMAS, (w["half"] + 1) * SHIFT_DMAS))
                            pe.wait_ge(exp_done, before("SCORE", w, 1, 1))
                            pe.matmul(score_ps[:, w["before"].get("SCORE", 0) % 2, c:HALF],
                                      ks[:, w["g"], w["h"], P * w["kt"]:P * (w["kt"] + 1)],
                                      qs[:, w["g"], w["h"], HALF * w["half"] + c:HALF * (w["half"] + 1)],
                                      start=True, stop=True).then_inc(score_filled, 1)
                        if kind == "VALUE":
                            c = first_column(w["half"], w["kt"])
                            if w["kt"] == 0:
                                pe.wait_ge(o_evacuated, before("EVAC", w, 1, 1))
                            pe.wait_ge(exp_done, before("VALUE", w, GROUP, GROUP + 2))
                            if diagonal(w["half"], w["kt"]):
                                pe.wait_ge(masked, before("DIAGONAL", w, 1, 1))
                            for h in range(GROUP):
                                ins = pe.matmul(o_ps[32 * h:32 * h + VW, w["half"], c:HALF], v[:, w["g"], w["kt"], h, :],
                                                prob[:, w["before"].get("VALUE", 0) % 2, h, c:HALF],
                                                start=w["kt"] == 0, stop=w["last"])
                            ins.then_inc(value_done, 1)
                        if kind == "SUMS":
                            pe.wait_ge(o_evacuated, before("EVAC", w, 1, NH))
                            for t in range(4):
                                ins = pe.matmul(side_ps[:, GROUP * t:GROUP * (t + 1)], on[:, w["g"], HALF * w["half"] + P * t:HALF * w["half"] + P * (t + 1)],
                                                pick[:, :], start=True, stop=True)
                            ins.then_inc(side_filled, 1)
                        if kind == "NORM":
                            pe.wait_ge(sums_spread, before("NORM", w, 1, 1))
                            for t in range(4):
                                ins = transpose(side_ps[:, P * t:P * (t + 1)],
                                                rsum_b[:, t, :, :].rearrange("p h c -> p (h c)"), ident[:, :])
                            ins.then_inc(side_filled, 1)
                        if kind == "OUT":
                            for t in range(2):
                                i = 2 * w["pair"] + t
                                for g in range(G):
                                    ins = pe.matmul(side_ps[:, D * t:D * (t + 1)], on[:, g, P * i:P * (i + 1)],
                                                    wo_sb[:, g, :], start=g == 0, stop=g == G - 1)
                            ins.then_inc(side_filled, 1)

                run(pe, work)

        nrm = keep("nrm", [P, B * TT, D], f32)
        row_stats = keep("row_stats", [P, B * TT, nc.vector.BN_STATS_DIM], f32)
        channel = ExitStack()
        with channel:
            def sb(name, shape, dt=f32):
                return channel.enter_context(nc.sbuf_tensor(name, shape, dt))

            def pb(name, shape):
                return channel.enter_context(nc.psum_tensor(name, shape, f32))

            def sem(name):
                return channel.enter_context(nc.semaphore(name))

            wq_sb = sb("wq2_sb", [KD + 1, KT, D])
            wk_sb = sb("wk2_sb", [KD + 1, KT, D])
            wvT_sb = sb("wvT2_sb", [KD, KT, D + 1])
            w2_sb = sb("w2_sb", [KD + 1, KT, D])
            x = sb("x_rows", [P, TT, D + 1])
            xT = sb("xT2", [KD + 1, KT, N])
            gram = sb("gram", [KD + 1, KT, D + 1])
            mixed = sb("mixed", [KD + 1, KT, D])
            blocks = sb("blocks", [KD, KT, KD])
            s_masked = sb("s_masked", [KD, KT, KD])
            s_top = sb("s_top", [KD, KT])
            s_low = sb("s_low", [KD, KT, KD])
            s_exp = sb("s_exp", [KD, KT, KD])
            s_sum = sb("s_sum", [KD, KT])
            s_inv = sb("s_inv", [KD, KT])
            attend = sb("attend", [KD, KT, KD])
            attendT = sb("attendT", [KD, KT, KD])
            united = sb("united", [KD + 1, KT, 3, 64])
            rowsT = sb("rowsT", [KD + 1, KT, 64, 16])
            xt_ps = pb("xt2_ps", [P, 2, HALF])
            gram_ps = pb("gram_ps", [P, HALF])
            chain_ps = pb("chain_ps", [P, HALF])
            rows_ps = pb("rows_ps", [P, 2, HALF])
            out_ps = pb("out_ps", [P, 2, HALF])

            weights_in = sem("weights2_in")
            const_pool = sem("const2_pool")
            const_dve = sem("const2_dve")
            stats_done = sem("stats2a_done")
            rstd_done = sem("rstd2_done")
            ln_done = sem("ln2_done")
            kept = sem("kept")
            turned = sem("turned")
            turned_out = sem("turned_out")
            gram_filled = sem("gram_filled")
            gram_out = sem("gram_out")
            chain_filled = sem("chain_filled")
            chain_out = sem("chain_out")
            low_done = sem("low_done")
            exp2_done = sem("exp2_done")
            soft = sem("soft")
            rows_filled = sem("rows_filled")
            rows_out = sem("rows_out")
            out_filled = sem("out_filled")
            out_out = sem("out_out")
            out_stats = sem("out_stats")
            passed = {eng: sem(f"passed2_{name}") for name, eng in (("vector", nc.vector), ("gpsimd", nc.gpsimd))}
            block = channel.enter_context(nc.Block())

            def apart(eng):
                eng.sem_inc(passed[eng], 1)

            def run(eng, work):
                run_stretches(eng, work, HEAD_2, STRETCHES_2)

            def norm_batch(order, before, b, w):
                return (1 if w["before"].get("LN", 0) else 0) if order is HEAD_2 else b + 2

            @block.sync
            def _(sp):
                for dst, src in ((wq_sb, wq2), (wk_sb, wk2), (wvT_sb, wvT2), (w2_sb, w2)):
                    sp.dma_start(dst[:, :, :], src).then_inc(weights_in, 16)

            @block.gpsimd
            def _(pool):
                pool.memset(blocks[:, :, :], 0.0).then_inc(const_pool, 1)
                pool.wait_ge(const_pool, 1)
                heads = blocks[:, :, :].rearrange("p k (h d) -> p k h d", d=DH)
                pool.affine_select(out=heads, in_=heads, compare_op=ALU.is_ge, fill=NEG, base=0,
                                   pattern=[[0, KT], [-DH, KD // DH], [0, DH]], channel_multiplier=1).then_inc(const_pool, 1)
                pool.wait_ge(const_pool, 2)
                pool.affine_select(out=heads, in_=heads, compare_op=ALU.is_ge, fill=NEG, base=DH - 1,
                                   pattern=[[0, KT], [DH, KD // DH], [0, DH]], channel_multiplier=-1).then_inc(const_pool, 1)

                def work(order, before, b):
                    for kind, w in order.jobs:
                        if kind == "LN":
                            pool.wait_ge(stats_done, before("LN", w, 2 * TT, 2 * TT))
                            apart(pool)
                            pool.tensor_scalar(rstd[:, :], mean_var[:, :, 1], LN_EPS, None, ALU.add).then_inc(rstd_done, 1)
                            pool.wait_ge(rstd_done, before("LN", w, 2, 1))
                            pool.tensor_tensor(rstd[:, :], rstd[:, :], minus_half[:, :], ALU.pow).then_inc(rstd_done, 1)
                            pool.wait_ge(ln_done, before("LN", w, TT, TT))
                            apart(pool)
                            pool.tensor_copy(nrm[:, bass.ds(TT * norm_batch(order, before, b, w), TT), :],
                                             x[:, :, 0:D]).then_inc(kept, 1)

                run(pool, work)

            @block.scalar
            def _(act):
                act.sem_inc(turned_out, 2)
                act.sem_inc(gram_out, 1)
                act.sem_inc(rows_out, 2)

                def work(order, before, b):
                    for kind, w in order.jobs:
                        if kind == "XT":
                            act.wait_ge(turned, before("XT", w, 1, 1))
                            act.activation(xT[0:KD, w["k"], HALF * w["half"]:HALF * (w["half"] + 1)],
                                           xt_ps[0:KD, w["half"], :], ACT.Copy).then_inc(turned_out, 1)
                        if kind == "GRAM":
                            act.wait_ge(gram_filled, before("GRAM", w, 1, 1))
                            act.activation(gram[0:TALL[w["i"]], w["i"], :], gram_ps[0:TALL[w["i"]], 0:D + 1],
                                           ACT.Copy).then_inc(gram_out, 1)
                        if kind == "SCORES":
                            act.wait_ge(low_done, before("SCORES", w, 1, 1))
                            act.activation(s_exp[:, :, :], s_low[:, :, :], ACT.Exp, scale=CHANNEL_SCALE).then_inc(exp2_done, 1)
                        if kind == "ROWS":
                            act.wait_ge(rows_filled, before("ROWS", w, 1, 1))
                            act.activation(rowsT[0:KD, w["a"], :, 8 * w["half"]:8 * (w["half"] + 1)].rearrange("p q s -> p s q"),
                                           rows_ps[0:KD, w["half"], :].rearrange("p (s q) -> p s q", q=64),
                                           ACT.Copy).then_inc(rows_out, 1)

                run(act, work)

            @block.vector
            def _(dve):
                dve.memset(x[:, :, D:D + 1], 1.0).then_inc(const_dve, 1)
                dve.memset(xT[KD:KD + 1, :, :], 1.0).then_inc(const_dve, 1)
                dve.memset(rowsT[KD:KD + 1, :, :, :], 1.0).then_inc(const_dve, 1)
                dve.sem_inc(chain_out, 1)
                dve.sem_inc(out_out, 2)
                dve.wait_ge(const_pool, 3)

                def row(t, i):
                    return t[:, bass.ds(i, 1), :].rearrange("p a d -> p (a d)")

                def work(order, before, b):
                    for kind, w in order.jobs:
                        if kind == "LN":
                            nb = norm_batch(order, before, b, w)
                            for t in range(TT):
                                dve.bn_stats(stat[:, t, :], row(hid, TT * nb + t)).then_inc(stats_done, 1)
                            dve.wait_ge(stats_done, before("LN", w, 2 * TT, TT))
                            apart(dve)
                            for t in range(TT):
                                dve.bn_aggr(mean_var[:, t, :], stat[:, t, :]).then_inc(stats_done, 1)
                            wait(dve, turned, before("XT", w))
                            wait(dve, kept, before("LN", w))
                            dve.wait_ge(rstd_done, before("LN", w, 2, 2))
                            for t in range(TT):
                                dve.tensor_scalar(x[:, t, 0:D], row(hid, TT * nb + t), mean_var[:, t, 0:1],
                                                  rstd[:, t:t + 1], ALU.subtract, ALU.mult).then_inc(ln_done, 1)
                        if kind == "MIX":
                            dve.wait_ge(chain_filled, before("MIX", w, 4, 1))
                            for k in range(KT):
                                ins = dve.tensor_copy(mixed[0:TALL[k], k, :], chain_ps[0:TALL[k], D * k:D * (k + 1)])
                            ins.then_inc(chain_out, 1)
                        if kind == "SCORES":
                            dve.wait_ge(chain_filled, before("SCORES", w, 4, 2))
                            s_ps = chain_ps[0:KD, 0:D].rearrange("p (m e) -> p m e", m=KT)
                            dve.tensor_tensor(s_masked[:, :, :], s_ps, blocks[:, :, :], ALU.add).then_inc(chain_out, 1)
                            dve.wait_ge(chain_out, before("SCORES", w, 4, 3))
                            dve.tensor_reduce(s_top[:, :], s_masked[:, :, :], AX.X, ALU.max).then_inc(soft, 1)
                            dve.wait_ge(soft, before("SCORES", w, 4, 1))
                            dve.tensor_tensor(s_low[:, :, :], s_masked[:, :, :], s_top[:, :].unsqueeze(2).to_broadcast([KD, KT, KD]),
                                              ALU.subtract).then_inc(low_done, 1)
                            dve.wait_ge(exp2_done, before("SCORES", w, 1, 1))
                            dve.tensor_reduce(s_sum[:, :], s_exp[:, :, :], AX.X, ALU.add).then_inc(soft, 1)
                            dve.wait_ge(soft, before("SCORES", w, 4, 2))
                            dve.reciprocal(s_inv[:, :], s_sum[:, :]).then_inc(soft, 1)
                            dve.wait_ge(soft, before("SCORES", w, 4, 3))
                            dve.tensor_tensor(attend[:, :, :], s_exp[:, :, :], s_inv[:, :].unsqueeze(2).to_broadcast([KD, KT, KD]),
                                              ALU.mult).then_inc(soft, 1)
                        if kind == "TURN":
                            dve.wait_ge(chain_filled, before("TURN", w, 4, 3))
                            dve.tensor_copy(attendT[:, :, :], chain_ps[0:KD, 0:D].rearrange("p (m c) -> p m c", m=KT)).then_inc(chain_out, 1)
                        if kind == "UNITE":
                            dve.wait_ge(chain_filled, before("UNITE", w, 4, 4))
                            for k in range(KT):
                                ins = dve.tensor_copy(united[0:TALL[k], k, :, :],
                                                      chain_ps[0:TALL[k], D * k:D * (k + 1)].rearrange("p (q r) -> p r q", r=3))
                            ins.then_inc(chain_out, 1)
                        if kind == "OUT":
                            if w["pair"] == 0:
                                dve.wait_ge(kept, before("MIX", w))
                            dve.wait_ge(out_filled, before("OUT", w, 1, 1))
                            rows = nrm[:, bass.ds(TT * b + 2 * w["pair"], 2), :]
                            dve.tensor_tensor(rows, out_ps[:, w["pair"] % 2, 0:2 * D].rearrange("p (t d) -> p t d", d=D), rows,
                                              ALU.add).then_inc(out_out, 1)
                            dve.wait_ge(out_out, before("OUT", w, 1, 3))
                            for t in range(2):
                                dve.bn_stats(row(row_stats, TT * b + 2 * w["pair"] + t),
                                             row(nrm, TT * b + 2 * w["pair"] + t)).then_inc(out_stats, 1)

                run(dve, work)
                dve.wait_ge(out_stats, B * TT)

            @block.tensor
            def _(pe):
                pe.wait_ge(weights_in, 16 * 4)
                pe.wait_ge(const_dve, 3)

                def transpose(out, in_, one):
                    return pe.matmul(out, in_, one, is_transpose=True, start=True, stop=True)

                def tile(k):
                    return slice(KD * k, KD * k + TALL[k])

                def work(order, before, b):
                    for kind, w in order.jobs:
                        if kind == "GRAM":
                            if w["i"] == 0:
                                pe.wait_ge(ln_done, before("GRAM", w, TT // 2, TT))
                            pe.wait_ge(gram_out, before("GRAM", w, 1, 1))
                            for t in range(TT):
                                ins = pe.matmul(gram_ps[0:TALL[w["i"]], 0:D + 1], x[:, t, tile(w["i"])], x[:, t, :],
                                                start=t == 0, stop=t == TT - 1)
                            ins.then_inc(gram_filled, 1)
                        if kind == "XT":
                            pe.wait_ge(turned_out, before("XT", w, 1, 1))
                            for t in range(4):
                                ins = transpose(xt_ps[0:KD, w["half"], P * t:P * (t + 1)],
                                                x[:, 4 * w["half"] + t, KD * w["k"]:KD * (w["k"] + 1)], ident[:, :])
                            ins.then_inc(turned, 1)
                        if kind == "MIX":
                            pe.wait_ge(gram_out, before("MIX", w, KT, KT + 1))
                            pe.wait_ge(chain_out, before("MIX", w, 4, 1))
                            for i in range(KT):
                                for k in range(KT):
                                    ins = pe.matmul(chain_ps[0:TALL[i], D * i:D * (i + 1)], gram[0:TALL[k], k, tile(i)],
                                                    wk_sb[0:TALL[k], k, :], start=k == 0, stop=k == KT - 1)
                            ins.then_inc(chain_filled, 1)
                        if kind == "SCORES":
                            pe.wait_ge(chain_out, before("SCORES", w, 4, 2))
                            for m in range(KT):
                                for k in range(KT):
                                    ins = pe.matmul(chain_ps[0:KD, KD * m:KD * (m + 1)], wq_sb[0:TALL[k], k, KD * m:KD * (m + 1)],
                                                    mixed[0:TALL[k], k, KD * m:KD * (m + 1)], start=k == 0, stop=k == KT - 1)
                            ins.then_inc(chain_filled, 1)
                        if kind == "TURN":
                            pe.wait_ge(soft, before("TURN", w, 4, 4))
                            pe.wait_ge(chain_out, before("TURN", w, 4, 3))
                            for m in range(KT):
                                ins = transpose(chain_ps[0:KD, KD * m:KD * (m + 1)], attend[:, m, :], ident[0:KD, 0:KD])
                            ins.then_inc(chain_filled, 1)
                        if kind == "UNITE":
                            pe.wait_ge(chain_out, before("UNITE", w, 4, 4))
                            for k in range(KT):
                                for m in range(KT):
                                    ins = pe.matmul(chain_ps[0:TALL[k], D * k + KD * m:D * k + KD * (m + 1)],
                                                    wvT_sb[:, m, tile(k)], attendT[:, m, :], start=True, stop=True)
                            ins.then_inc(chain_filled, 1)
                        if kind == "ROWS":
                            if w["a"] == 0 and w["half"] == 0:
                                pe.wait_ge(chain_out, before("UNITE", w, 4, 1))
                                pe.wait_ge(turned_out, before("XT", w, 1, 2))
                            pe.wait_ge(rows_out, before("ROWS", w, 1, 1))
                            for s in range(8 * w["half"], 8 * (w["half"] + 1)):
                                q0 = 64 * (s - 8 * w["half"])
                                for first, count, r, token in pieces(D * s + RUN * w["a"]):
                                    for k in range(KT):
                                        ins = pe.matmul(rows_ps[first:first + count, w["half"], q0:q0 + 64],
                                                        xT[0:TALL[k], k, token:token + count],
                                                        united[0:TALL[k], k, r, :], start=k == 0, stop=k == KT - 1)
                            ins.then_inc(rows_filled, 1)
                        if kind == "OUT":
                            if w["pair"] == 0:
                                pe.wait_ge(rows_out, before("ROWS", w, 1, 2))
                            pe.wait_ge(out_out, before("OUT", w, 1, 1))
                            for t in range(2):
                                for a in range(KT):
                                    cols = rowsT[0:TALL[a], a, 8 * (2 * w["pair"] + t):8 * (2 * w["pair"] + t + 1), :]
                                    ins = pe.matmul(out_ps[:, w["pair"] % 2, D * t:D * (t + 1)], cols.rearrange("p q s -> p (q s)"),
                                                    w2_sb[0:TALL[a], a, :], start=a == 0, stop=a == KT - 1)
                            ins.then_inc(out_filled, 1)

                run(pe, work)

        moe = ExitStack()
        with moe:
            def sb(name, shape, dt=f32):
                return moe.enter_context(nc.sbuf_tensor(name, shape, dt))

            def pb(name, shape):
                return moe.enter_context(nc.psum_tensor(name, shape, f32))

            def sem(name):
                return moe.enter_context(nc.semaphore(name))

            ROWS = B * TT
            stats = row_stats
            COUNT = B * N * D
            HT = TOP * FT
            fc = sb("fc", [KD, 2, TOP, KT, F])
            pj = sb("pj", [P, 2, TOP, FT, D])
            fcb = sb("fcb", [P, 2, TOP, FT])
            pjb = sb("pjb", [P, 2, TOP, D])
            pj_bias = sb("pj_bias", [P, 2, D])
            bias_0 = sb("bias_0", [P, D])
            act_h = sb("act_h", [P, HT, HALF])
            x1 = sb("x1", [P, 2, TT, D])
            x1T = sb("x1T", [KD, KT, N])
            ln_b = sb("ln_b", [P, 4, D])
            ln_f = sb("ln_f", [KD, 2, KT])
            rw = sb("rw", [KD, KT, E])
            rb = sb("rb", [B, E])
            moments = sb("moments", [P, 2, 2])
            overall = sb("overall", [P, 2, 8])
            spread = sb("spread", [P, 2, 2])
            average = sb("average", [P, P])
            one_row = sb("one_row", [1, P])
            batch_row = sb("batch_row", [P, B, B])
            a_b = sb("a_b", [P, D])
            c_b = sb("c_b", [P, D])
            a_f = sb("a_f", [KD, KT])
            a_n = sb("a_n", [KD, KT])
            c_f = sb("c_f", [KD, KT])
            ysum = sb("ysum", [B, D])
            xmean = sb("xmean", [KD, KT, B])
            logits = sb("logits", [B, E])
            negtop = sb("negtop", [B, 1])
            expo = sb("expo", [B, E])
            total = sb("total", [B, 1])
            rtotal = sb("rtotal", [B, 1])
            gate = sb("gate", [B, E])
            best = sb("best", [B, E])
            which = sb("which", [B, E], u32)
            best_row = sb("best_row", [1, B * TOP])
            which_row = sb("which_row", [1, B * TOP], u32)
            gates = sb("gates", [P, B * TOP])

            fc_ps = pb("fc_ps", [P, 4, HALF])
            z_ps = pb("z_ps", [P, 2, HALF])
            xt_ps = pb("xt_ps", [P, 2, HALF])

            consts_in = sem("consts_in")
            const_done = sem("const_done")
            weights_in = [sem("weights_even"), sem("weights_odd")]
            small = sem("small")
            small_pe = sem("small_pe")
            small_pool = sem("small_pool")
            small_act = sem("small_act")
            rows_in = sem("rows_in")
            scaled = sem("scaled")
            x1_half = sem("x1_half")
            x1_done = sem("x1_done")
            bias_half = sem("bias_half")
            bias_done = sem("bias_done")
            x1_kept = sem("x1_kept")
            xt_filled = sem("xt_filled")
            xt_drained = sem("xt_drained")
            fc_filled = sem("fc_filled")
            gelu_done = sem("gelu_done")
            z_filled = sem("z_filled")
            z_drained = sem("z_drained")
            stats2_done = sem("stats2_done")
            finished = sem("finished")
            final_1 = sem("final_1")
            final_2 = sem("final_2")
            written = sem("written")
            passed = sem("passed")

            LOADS = 16 * 4 * TOP
            block = moe.enter_context(nc.Block())

            class Batch:

                def __init__(self, pair, odd):
                    self.pair, self.odd = pair, odd

                def times(self, each, more=0):
                    return self.pair * (2 * each) + (self.odd * each + more)

            def by_batch(eng, work):
                with eng.Fori(0, B // 2 - 1) as pair:
                    for odd in range(2):
                        work(Batch(pair, odd), True)
                for odd in range(2):
                    work(Batch(B // 2 - 1, odd), odd == 0)

            @block.sync
            def _(sp):
                for i in range(4):
                    sp.dma_start(ln_b[:, i, :], ln[i].partition_broadcast(P)).then_inc(consts_in, 16)
                sp.dma_start(ln_f[:, :, :], ln_cols).then_inc(consts_in, 16)
                sp.dma_start(rw[:, :, :], r_w.rearrange("(k p) e -> p k e", p=KD)).then_inc(consts_in, 16)
                sp.dma_start(rb[:, :], r_b.partition_broadcast(B)).then_inc(consts_in, 16)
                sp.wait_ge(small, CHOSEN)
                sp.dma_start(best_row[:, :], best[:, 0:TOP]).then_inc(rows_in, 16)
                sp.dma_start(which_row[:, :], which[:, 0:TOP]).then_inc(rows_in, 16)
                sp.wait_ge(rows_in, 32)

                def load(batch, parity):
                    for c in range(TOP):
                        e = sp.value_load(which_row[0:1, bass.ds(batch.times(TOP, c), 1)], min_val=0, max_val=E - 1)
                        sp.dma_start(fc[:, parity, c, :, :], fc_w[bass.ds(e, 1), :, :].rearrange("a (k p) f -> p (a k) f", p=KD)).then_inc(weights_in[parity], 16)
                        sp.dma_start(pj[:, parity, c, :, :], pj_w[bass.ds(e, 1), :, :].rearrange("a (t p) d -> p (a t) d", p=P)).then_inc(weights_in[parity], 16)
                        sp.dma_start(fcb[:, parity, c, :], fc_b[bass.ds(e, 1), :, :].rearrange("a p t -> p (a t)")).then_inc(weights_in[parity], 16)
                        sp.dma_start(pjb[:, parity, c, :], pj_b[bass.ds(e, 1), :].rearrange("a d -> (a d)").partition_broadcast(P)).then_inc(weights_in[parity], 16)

                def work(batch, more):
                    if more:
                        sp.wait_ge(bias_done, batch.times(1, 1))
                        sp.sem_inc(passed, 1)
                        nxt = Batch(batch.pair, 1) if batch.odd == 0 else Batch(batch.pair + 1, 0)
                        load(nxt, 1 - batch.odd)

                load(Batch(0, 0), 0)
                by_batch(sp, work)
                for b in range(B):
                    sp.wait_ge(final_2, b + 1)
                    sp.dma_start(out[b].rearrange("(t p) d -> p t d", p=P), nrm[:, TT * b:TT * (b + 1), :]).then_inc(written, 16)
                sp.wait_ge(written, 16 * B)

            @block.gpsimd
            def _(pool):
                pool.memset(average[:, :], 1.0 / P).then_inc(const_done, 1)
                pool.memset(one_row[:, :], 1.0).then_inc(const_done, 1)
                pool.memset(batch_row[:, :, :], 0.0).then_inc(const_done, 1)
                pool.wait_ge(const_done, 3)
                pool.affine_select(out=batch_row[:, :, :], in_=batch_row[:, :, :], compare_op=ALU.not_equal, fill=1.0,
                                   base=0, pattern=[[1, B], [-1, B]], channel_multiplier=0).then_inc(const_done, 1)

                def inverse_root(norm):
                    pool.tensor_tensor(overall[:, norm, 4:5], overall[:, norm, 3:4], minus_half[:, 0:1], ALU.pow).then_inc(small_pool, 1)

                pool.wait_ge(small, VARIANCE)
                inverse_root(0)

                def work(batch, more):
                    pool.wait_ge(x1_done, batch.times(1, 1))
                    pool.wait_ge(bias_done, batch.times(1, 1))
                    pool.tensor_tensor(nrm[:, bass.ds(batch.times(TT), TT), :], x1[:, batch.odd, :, :],
                                       pj_bias[:, batch.odd, :].unsqueeze(1).to_broadcast([P, TT, D]), ALU.add).then_inc(x1_kept, 1)
                    pool.wait_ge(stats2_done, batch.times(TT, TT))
                    rows = nrm[:, bass.ds(batch.times(TT), TT), :]
                    pool.tensor_tensor(rows, rows, ln_b[:, 2, :].unsqueeze(1).to_broadcast([P, TT, D]), ALU.mult).then_inc(finished, 1)
                    rows = hid[:, bass.ds(batch.times(TT), TT), :]
                    pool.tensor_tensor(rows, rows, ln_b[:, 3, :].unsqueeze(1).to_broadcast([P, TT, D]), ALU.add).then_inc(finished, 1)

                pool.wait_ge(consts_in, 16 * 7)
                by_batch(pool, work)
                pool.wait_ge(small, VARIANCE_2)
                inverse_root(1)
                pool.wait_ge(small, ADDEND)
                for b in range(B):
                    pool.wait_ge(final_1, b + 1)
                    rows = nrm[:, TT * b:TT * (b + 1), :]
                    pool.tensor_tensor(rows, rows, c_b[:, :].unsqueeze(1).to_broadcast([P, TT, D]), ALU.add).then_inc(final_2, 1)

            @block.scalar
            def _(act):
                act.sem_inc(gelu_done, 4)
                act.sem_inc(xt_drained, 2)
                act.wait_ge(small, NEGTOP)
                act.activation(expo[:, :], logits[:, :], ACT.Exp, bias=negtop[:, 0:1], accum_out=total[:, 0:1]).then_inc(small_act, 1)

                def turn(first):
                    for k in range(KT):
                        for half in range(NH):
                            act.wait_ge(xt_filled, first + (NH * k + half + 1))
                            act.activation(x1T[:, k, HALF * half:HALF * (half + 1)], xt_ps[0:KD, half, :],
                                           ACT.Copy).then_inc(xt_drained, 1)

                def work(batch, more):
                    act.wait_ge(weights_in[batch.odd], batch.pair * LOADS + LOADS)
                    for half in range(NH):
                        for i in range(HT):
                            act.wait_ge(fc_filled, batch.times(NH * HT, HT * half + i + 1))
                            act.activation(act_h[:, i, :], fc_ps[:, i % 4, :], ACT.Gelu_apprx_tanh,
                                           bias=fcb[:, batch.odd, i // FT, i % FT:i % FT + 1]).then_inc(gelu_done, 1)
                    if more:
                        turn(batch.times(4, 4))

                turn(0)
                by_batch(act, work)

            count = [0]

            @block.vector
            def _(dve):
                dve.sem_inc(z_drained, 2)

                def mark(ins, name=None):
                    ins.then_inc(small, 1)
                    count[0] += 1
                    dve.wait_ge(small, count[0])
                    if name:
                        assert count[0] == name, (count[0], name)

                def global_norm(norm, pe_at, variance, negmean):
                    o = overall[:, norm, :]
                    mark(dve.bn_aggr(moments[:, norm, :], stats[:, :, :].rearrange("p r s -> p (r s)")))
                    dve.wait_ge(small_pe, pe_at)
                    mark(dve.tensor_copy(o[:, 0:2], xt_ps[:, norm, 0:2]))
                    mark(dve.tensor_tensor(spread[:, norm, 0:1], moments[:, norm, 0:1], o[:, 0:1], ALU.subtract))
                    mark(dve.tensor_tensor(spread[:, norm, 1:2], spread[:, norm, 0:1], spread[:, norm, 0:1], ALU.mult))
                    dve.wait_ge(small_pe, pe_at + 1)
                    mark(dve.tensor_tensor(o[:, 2:3], xt_ps[:, norm, 4:5], o[:, 1:2], ALU.add))
                    mark(dve.tensor_scalar(o[:, 3:4], o[:, 2:3], COUNT / (COUNT - 1.0), GLOBAL_EPS, ALU.mult, ALU.add), variance)
                    mark(dve.tensor_scalar(o[:, 5:6], o[:, 0:1], -1.0, None, ALU.mult), negmean)
                    dve.wait_ge(small_pool, norm + 1)

                dve.wait_ge(consts_in, 16 * 7)
                global_norm(0, 2, VARIANCE, VARIANCE + 1)
                o = overall[:, 0, :]
                mark(dve.tensor_scalar(a_b[:, :], ln_b[:, 0, :], o[:, 4:5], None, ALU.mult))
                mark(dve.scalar_tensor_tensor(c_b[:, :], a_b[:, :], o[:, 5:6], ln_b[:, 1, :], ALU.mult, ALU.add))
                mark(dve.tensor_scalar(a_f[:, :], ln_f[:, 0, :], o[0:KD, 4:5], None, ALU.mult))
                mark(dve.scalar_tensor_tensor(c_f[:, :], a_f[:, :], o[0:KD, 5:6], ln_f[:, 1, :], ALU.mult, ALU.add))
                mark(dve.tensor_scalar(a_n[:, :], a_f[:, :], 1.0 / N, None, ALU.mult))
                mark(dve.tensor_copy(ysum[:, :], fc_ps[0:B, 0, 0:D]), YSUM)
                dve.wait_ge(small_pe, 4)
                for k in range(KT):
                    mark(dve.tensor_scalar(xmean[:, k, :], fc_ps[0:KD, 1, B * k:B * (k + 1)], a_n[:, k:k + 1], c_f[:, k:k + 1],
                                           ALU.mult, ALU.add), XMEAN - KT + 1 + k)
                dve.wait_ge(small_pe, 5)
                mark(dve.tensor_tensor(logits[:, :], fc_ps[0:B, 2, 0:E], rb[:, :], ALU.add))
                mark(dve.tensor_reduce(negtop[:, 0:1], logits[:, :], AX.X, ALU.max, negate=True), NEGTOP)
                dve.wait_ge(small_act, 1)
                mark(dve.reciprocal(rtotal[:, :], total[:, :]))
                mark(dve.tensor_scalar(gate[:, :], expo[:, :], rtotal[:, 0:1], None, ALU.mult))
                mark(dve.max(best[:, :], gate[:, :]))
                mark(dve.max_index(which[:, :], best[:, :], gate[:, :]), CHOSEN)

                def work(batch, more):
                    p = batch.odd
                    dve.wait_ge(weights_in[p], batch.pair * LOADS + LOADS)
                    for c in range(TOP):
                        g = gates[:, bass.ds(batch.times(TOP, c), 1)]
                        dve.tensor_scalar(pj[:, p, c, :, :], pj[:, p, c, :, :], g, None, ALU.mult).then_inc(scaled, 1)
                    dve.tensor_scalar(bias_0[:, :], pjb[:, p, 0, :], gates[:, bass.ds(batch.times(TOP), 1)], None, ALU.mult).then_inc(bias_half, 1)
                    dve.wait_ge(bias_half, batch.times(1, 1))
                    dve.scalar_tensor_tensor(pj_bias[:, p, :], pjb[:, p, 1, :], gates[:, bass.ds(batch.times(TOP, 1), 1)],
                                             bias_0[:, :], ALU.mult, ALU.add).then_inc(bias_done, 1)
                    if more:
                        next_x1(1 - p, batch.times(1, 1), batch.times(TT, TT), batch.times(1, 1))
                    for half in range(NH):
                        for pair in range(2):
                            i = 2 * half + pair
                            if i == 0:
                                dve.wait_ge(x1_kept, batch.times(1, 1))
                            dve.wait_ge(z_filled, batch.times(4, i + 1))
                            rows = nrm[:, bass.ds(batch.times(TT, 2 * i), 2), :]
                            dve.tensor_tensor(rows, z_ps[:, i % 2, 0:2 * D].rearrange("p (t d) -> p t d", d=D), rows,
                                              ALU.add).then_inc(z_drained, 1)
                            dve.wait_ge(z_drained, batch.times(4, i + 3))
                            for t in range(2):
                                r = batch.times(TT, 2 * i + t)
                                dve.bn_stats(stats[:, bass.ds(r, 1), :].rearrange("p a s -> p (a s)"),
                                             nrm[:, bass.ds(r, 1), :].rearrange("p a d -> p (a d)")).then_inc(stats2_done, 1)

                def next_x1(parity, number, first, kept):
                    if kept is not None:
                        dve.wait_ge(x1_kept, kept)
                    x = x1[:, parity, :, :]
                    dve.tensor_tensor(x, nrm[:, bass.ds(first, TT), :], a_b[:, :].unsqueeze(1).to_broadcast([P, TT, D]),
                                      ALU.mult).then_inc(x1_half, 1)
                    dve.wait_ge(x1_half, number + 1)
                    dve.tensor_tensor(x, x, c_b[:, :].unsqueeze(1).to_broadcast([P, TT, D]), ALU.add).then_inc(x1_done, 1)

                next_x1(0, 0, 0, None)
                dve.wait_ge(small_pe, 6)
                mark(dve.tensor_copy(gates[:, :], fc_ps[:, 3, 0:B * TOP]), GATES)
                by_batch(dve, work)
                dve.wait_ge(stats2_done, ROWS)
                global_norm(1, 7, VARIANCE_2, VARIANCE_2 + 1)
                o = overall[:, 1, :]
                mark(dve.tensor_scalar(a_b[:, :], ln_b[:, 2, :], o[:, 4:5], None, ALU.mult))
                mark(dve.tensor_scalar(c_b[:, :], a_b[:, :], o[:, 5:6], None, ALU.mult), ADDEND)
                dve.wait_ge(finished, 2 * B)
                for b in range(B):
                    rows = slice(TT * b, TT * (b + 1))
                    dve.scalar_tensor_tensor(nrm[:, rows, :], nrm[:, rows, :], o[:, 4:5], hid[:, rows, :],
                                             ALU.mult, ALU.add).then_inc(final_1, 1)

            @block.tensor
            def _(pe):
                def transpose(out, in_, one):
                    return pe.matmul(out, in_, one, is_transpose=True, start=True, stop=True)

                pe.wait_ge(const_done, 4)
                pe.wait_ge(consts_in, 16 * 7)
                for b in range(B):
                    for t in range(TT):
                        ins = pe.matmul(fc_ps[0:B, 0, 0:D], batch_row[:, b, :], nrm[:, TT * b + t, :],
                                            start=b == 0 and t == 0, stop=b == B - 1 and t == TT - 1)
                ins.then_inc(small_pe, 1)

                def averages(norm, moments_at):
                    pe.wait_ge(small, moments_at)
                    pe.matmul(xt_ps[:, norm, 0:2], average[:, :], moments[:, norm, :], start=True, stop=True).then_inc(small_pe, 1)
                    pe.wait_ge(small, moments_at + 3)
                    pe.matmul(xt_ps[:, norm, 4:5], average[:, :], spread[:, norm, 1:2], start=True, stop=True).then_inc(small_pe, 1)

                averages(0, MOMENTS)
                pe.wait_ge(small, YSUM)
                for k in range(KT):
                    ins = transpose(fc_ps[0:KD, 1, B * k:B * (k + 1)], ysum[:, KD * k:KD * (k + 1)], ident[0:B, 0:B])
                ins.then_inc(small_pe, 1)
                pe.wait_ge(small, XMEAN)
                for k in range(KT):
                    ins = pe.matmul(fc_ps[0:B, 2, 0:E], xmean[:, k, :], rw[:, k, :], start=k == 0, stop=k == KT - 1)
                ins.then_inc(small_pe, 1)
                pe.wait_ge(rows_in, 32)
                pe.matmul(fc_ps[:, 3, 0:B * TOP], one_row[:, :], best_row[:, :], start=True, stop=True).then_inc(small_pe, 1)

                def turn(parity, x1_at, first):
                    pe.wait_ge(x1_done, x1_at)
                    for k in range(KT):
                        for half in range(NH):
                            pe.wait_ge(xt_drained, first + (NH * k + half + 1))
                            for t in range(4):
                                ins = transpose(xt_ps[0:KD, half, P * t:P * (t + 1)],
                                                x1[:, parity, 4 * half + t, KD * k:KD * (k + 1)], ident[:, :])
                            ins.then_inc(xt_filled, 1)

                def work(batch, more):
                    p = batch.odd
                    pe.wait_ge(weights_in[p], batch.pair * LOADS + LOADS)
                    for half in range(NH):
                        if half == 0:
                            pe.wait_ge(xt_drained, batch.times(4, 6))
                        for i in range(HT):
                            pe.wait_ge(gelu_done, batch.times(NH * HT, HT * half + i + 1))
                            for k in range(KT):
                                ins = pe.matmul(fc_ps[:, i % 4, :], fc[:, p, i // FT, k, P * (i % FT):P * (i % FT + 1)],
                                                x1T[:, k, HALF * half:HALF * (half + 1)], start=k == 0, stop=k == KT - 1)
                            ins.then_inc(fc_filled, 1)
                        if half == NH - 1 and more:
                            turn(1 - p, batch.times(1, 2), batch.times(4, 4))
                        pe.wait_ge(scaled, batch.times(TOP, TOP))
                        pe.wait_ge(gelu_done, batch.times(NH * HT, HT * (half + 1) + 4))
                        for pair in range(2):
                            pe.wait_ge(z_drained, batch.times(4, 2 * half + pair + 1))
                            for t in range(2):
                                c = 2 * pair + t
                                for i in range(HT):
                                    ins = pe.matmul(z_ps[:, pair, D * t:D * (t + 1)], act_h[:, i, P * c:P * (c + 1)],
                                                    pj[:, p, i // FT, i % FT, :], start=i == 0, stop=i == HT - 1)
                            ins.then_inc(z_filled, 1)

                pe.wait_ge(small, GATES)
                turn(0, 1, 0)
                by_batch(pe, work)
                averages(1, MOMENTS_2)


INPUTS = ("tok", "table", "wqk", "wv", "wo", "wk2", "wq2", "wvT2", "w2", "r_w", "r_b", "fc_w", "fc_b", "pj_w", "pj_b", "ln", "ln_cols")


def layout(given):
    import numpy as np

    out = {}
    ids = np.asarray(given["x"])
    out["tok"] = np.ascontiguousarray(ids.reshape(B * TT, P).T)
    out["table"] = np.asarray(given["L0_tok_weight"])
    q, k, v, o = (np.asarray(given["L0_attn_" + n]).T for n in ("Wq", "Wk", "Wv", "Wo"))

    def by_group(w):
        return w.reshape(D, G, GROUP, DH).transpose(1, 0, 3, 2).reshape(G, D, GROUP * DH)

    both = np.concatenate([by_group(q), by_group(k)], axis=2)
    out["wqk"] = np.ascontiguousarray(both.reshape(G, KT, KD, P).transpose(2, 0, 1, 3))
    out["wv"] = np.ascontiguousarray(v.reshape(KT, KD, D).transpose(1, 0, 2))
    out["wo"] = np.zeros((P, G, D), o.dtype)
    for h in range(GROUP):
        out["wo"][32 * h:32 * h + DH] = o.reshape(G, GROUP, DH, D)[:, h].transpose(1, 0, 2)

    def tall(w, b):
        rows = np.zeros((KD + 1, KT, w.shape[1]), w.dtype)
        rows[:KD] = w.reshape(KT, KD, -1).transpose(1, 0, 2)
        rows[KD, 1] = b
        return rows

    w1, b1 = np.asarray(given["L0_ffn_W1_w"]), np.asarray(given["L0_ffn_W1_b"])
    out["wq2"] = tall(w1[:, :D], b1[:D])
    out["wk2"] = tall(w1[:, D:2 * D], b1[D:2 * D])
    out["wvT2"] = np.ascontiguousarray(np.concatenate([w1[:, 2 * D:], b1[None, 2 * D:]]).T.reshape(KT, KD, D + 1).transpose(1, 0, 2))
    out["w2"] = tall(np.asarray(given["L0_ffn_W2_w"]), np.asarray(given["L0_ffn_W2_b"]))
    for name, key in (("r_w", "r_w"), ("r_b", "r_b"), ("fc_w", "fc_w"), ("fc_b", "fc_b"), ("pj_w", "proj_w"), ("pj_b", "proj_b")):
        out[name] = np.asarray(given["L0_ffn_" + key])
    out["fc_b"] = np.ascontiguousarray(out["fc_b"].reshape(E, FT, P).transpose(0, 2, 1))
    norms = [np.asarray(given["L0_ffn_" + n]) for n in ("ln1_w", "ln1_b", "ln2_w", "ln2_b")]
    out["ln"] = np.stack(norms)
    out["ln_cols"] = np.ascontiguousarray(np.stack(norms[:2]).reshape(2, KT, KD).transpose(2, 0, 1))
    return out


def kernel(**inputs):
    import numpy as np
    import concourse.bacc as bacc
    from concourse.bass_utils import run_bass_kernel_spmd

    nc = bacc.Bacc("TRN2", target_bir_lowering=False, num_devices=1)
    laid = layout(inputs)
    arrays, args = {}, []
    for name in INPUTS:
        a = np.ascontiguousarray(laid[name])
        arrays[f"in_{name}"] = a
        args.append(nc.dram_tensor(f"in_{name}", a.shape, mybir.dt.from_np(a.dtype), kind="ExternalInput").ap())
    args.append(nc.dram_tensor("out_rows", (B, N, D), mybir.dt.float32, kind="ExternalOutput").ap())
    build(nc, *args)
    done = run_bass_kernel_spmd(nc, [arrays], core_ids=[0])
    return done.results[0]["out_rows"]
```

```python
import concourse.bass as bass
from concourse import mybir
from contextlib import ExitStack

B, N, D = 8, 1024, 192
HEADS, DH = 12, 16
P = 128
GROUP = 4
G = HEADS // GROUP
TT = N // P
HALF = 512
NH = N // HALF
KD = 96
KT = D // KD
SLOTS = 6
STACK = SLOTS * DH
SHIFT = 2
VW = DH + 1
E, F = 8, 768
FT = F // P
TOP = 2
LAG = 1
PROBS, MAX_BANKS = 3, 3
NEG = -1.0e30
LOWEST = -3.0e38
LN_EPS, GLOBAL_EPS = 1e-5, 1e-12
SCORE_SCALE, CHANNEL_SCALE = DH ** -0.5, N ** -0.5
Q_PARTS = (0, 0, 1, 1, 0, 2)
K_PARTS = (0, 1, 0, 1, 2, 0)
TALL = (KD, KD + 1)
THIRD = D // 3
MOMENTS, VARIANCE = 1, 6
XMEAN, NEGTOP, CHOSEN, GATES = 14, 16, 20, 21
MOMENTS_2, VARIANCE_2, ADDEND = 22, 27, 30



def key_tiles(half):
    return range(4 * (half + 1))


def diagonal(half, kt):
    return kt // 4 == half


def first_column(half, kt):
    return max(0, P * kt - HALF * half)


def max_tiles(half):
    return [(t, h, c) for t in range(4 * half, 4 * half + 4) for h in range(GROUP) for c in range(t // 4 + 1)]


class Order:

    BANKED = {"QK": "prep", "V": "prep", "XT": "prep", "SHIFT": "side", "SUMS": "side", "NORM": "side", "OUT": "side"}

    def __init__(self):
        self.jobs, self.count, self.waiting = [], {}, []

    def add(self, kind, **what):
        self.jobs.append((kind, what | {"before": dict(self.count)}))
        self.tally(kind)
        if kind in self.BANKED:
            self.tally(self.BANKED[kind])

    def tally(self, kind):
        self.count[kind] = self.count.get(kind, 0) + 1


def max_jobs(o, g, half, ahead):
    for t, h, c in max_tiles(half):
        yield lambda t=t, h=h, c=c: o.add("MAX", g=g, t=t, h=h, c=c, ahead=ahead)
    yield lambda: o.add("NEGATE", g=g, half=half)


def step(o, g, maxi, prep, next_ln, outs):
    for half in range(NH):
        side = []
        if half == 0:
            if prep is not None:
                side += [(1, "QK", dict(g=prep, half=0)), (5, "PART", dict(g=prep, half=0)),
                         (5, "QK", dict(g=prep, half=1)), (9, "PART", dict(g=prep, half=1)),
                         (9, "STACK", dict(g=prep))]
            if g > 0 or outs:
                side += [(6, "SUMS", dict(g=(g - 1) % G, half=1)), (9, "SPREAD", {}), (12, "NORM", dict(g=(g - 1) % G, half=1))]
            side.append((3, "SHIFT", dict(g=g, half=1)))
            if next_ln:
                side += [(2 + 4 * i, "STAT", dict(i=i)) for i in range(4)]
        else:
            side += [(6, "SUMS", dict(g=g, half=0)), (9, "SPREAD", {})]
            if maxi is not None:
                side.append((2, "SHIFT", dict(g=maxi, half=0)))
            side.append((12, "NORM", dict(g=g, half=0)))
            if prep is not None:
                side.append((28 if g == 1 else 4, "VALUES", dict(g=prep)))
            if next_ln:
                side += [(3, "RSTD", {}), (6, "LN", {})]
                side += [(8 + 4 * (2 * k + i), "XT", dict(k=k, half=i)) for k in range(KT) for i in range(NH)]
            if g == 1 and prep is not None:
                side += [(8 + 4 * i, "V", dict(pair=i)) for i in range(4)]
            if g == 0 and outs:
                side += [(17 + 6 * i, "OUT", dict(pair=2 + i, late=True)) for i in range(2)]
            if g == G - 1:
                side += [(17 + 6 * i, "OUT", dict(pair=i, late=False)) for i in range(2)]
        side.sort(key=lambda job: job[0])
        kts = list(key_tiles(half))
        maxima = list(max_jobs(o, maxi, half, 1)) if maxi is not None else []
        every, slots = len(maxima), GROUP * len(kts)
        for i in range(len(kts)):
            for h in range(GROUP):
                o.add("SCORE", g=g, half=half, kt=kts[i], h=h)
                while every - len(maxima) < (GROUP * i + h + 1) * every // slots:
                    maxima.pop(0)()
                while side and side[0][0] == GROUP * i + h:
                    _, kind, what = side.pop(0)
                    o.add(kind, **what)
            o.tally("BLOCK")
            if diagonal(half, kts[i]):
                o.tally("DIAGONAL_SCORES")
            o.waiting.append(dict(g=g, half=half, kt=kts[i], last=i == len(kts) - 1))
            values(o, LAG)
        assert not side
    o.tally("UNIT")


def values(o, lag):
    while len(o.waiting) > lag:
        what = o.waiting.pop(0)
        o.add("VALUE", **what)
        if diagonal(what["half"], what["kt"]):
            o.tally("DIAGONAL")
        if what["last"]:
            o.add("EVAC", g=what["g"], half=what["half"])


def tail_order():
    o = Order()
    o.add("SUMS", g=G - 1, half=1)
    o.add("SPREAD")
    o.add("NORM", g=G - 1, half=1)
    for i in range(2, 4):
        o.add("OUT", pair=i, late=True)
    return o


def late(jobs, kinds):
    out, held = [], []
    if not any(job[0] == "SCORE" for job in jobs):
        return jobs
    for job in jobs:
        if job[0] in kinds:
            held.append([job, kinds[job[0]]])
            continue
        out.append(job)
        if job[0] == "SCORE":
            for h in held:
                h[1] -= 1
            while held and held[0][1] <= 0:
                out.append(held.pop(0)[0])
    return out + [job for job, _ in held]


def head_order():
    o = Order()
    for i in range(4):
        o.add("STAT", i=i)
    o.add("RSTD")
    o.add("LN")
    for k in range(KT):
        for i in range(NH):
            o.add("XT", k=k, half=i)
    for g in range(2):
        for i in range(NH):
            o.add("QK", g=g, half=i)
            o.add("PART", g=g, half=i)
        o.add("STACK", g=g)
        if g == 0:
            for i in range(4):
                o.add("V", pair=i)
        o.add("VALUES", g=g)
    for half in range(NH):
        for job in max_jobs(o, 0, half, 0):
            job()
    o.add("SHIFT", g=0, half=0)
    return o


def batch_order(first, last):
    o = Order()
    units = list(range(G)) + [None if last else g for g in range(G - 1)]
    for g in range(G):
        step(o, units[g], units[g + 1], units[g + 2], g == 0 and not last, g == 0 and not first)
    values(o, 0)
    return o


def channel_head():
    o = Order()
    o.add("STAT", u=0)
    o.add("LN", u=0)
    for i in range(KT):
        o.add("GRAM", i=i)
    for i in range(4):
        o.add("XT", k=i // NH, half=i % NH, u=0)
    o.add("STAT", u=1)
    o.add("LN", u=1)
    return o


def channel_pair(last):
    o = Order()
    for u in range(2):
        gram, norm = not (last and u), not last
        o.add("MIX", u=u)
        if norm:
            o.add("STAT", u=u + 2)
        if gram:
            o.add("GRAM", i=0)
        o.add("SCORES", u=u)
        if gram:
            o.add("GRAM", i=1)
            o.add("XT", k=0, half=0, u=1 - u)
        o.add("TURN", u=u)
        if gram:
            o.add("XT", k=0, half=1, u=1 - u)
        o.add("UNITE", u=u)
        for i in range(4):
            if gram and i < NH:
                o.add("XT", k=1, half=i, u=1 - u)
            o.add("ROWS", n=i, u=u)
        for i in range(4):
            o.add("OUT", pair=i, u=u)
            if norm and i == 1:
                o.add("LN", u=u + 2)
        o.add("FOLD", u=u)
    return o


def stretches(head, parts):
    out, start, first = [], dict(head.count), 0
    for order, times in parts:
        out.append((times if times > 1 else None, first, order, dict(start)))
        first += times
        for kind, n in order.count.items():
            start[kind] = start.get(kind, 0) + n * times
    return out


class Numbers:

    def __init__(self, start, per, loop, eng=None):
        self.start, self.per, self.loop, self.eng, self.held = start, per, loop, eng, {}

    def __call__(self, kind, what, each=1, more=0):
        fixed = each * (self.start.get(kind, 0) + what["before"].get(kind, 0)) + more
        per = each * self.per.get(kind, 0)
        if not per or isinstance(self.loop, int):
            return fixed
        if per not in self.held:
            self.held[per] = self.eng.snap(self.loop * per)
        return self.held[per] + fixed


def rows_of(n):
    for i in range(2):
        for upper in range(2):
            for r in range(3):
                s, third = divmod(N // 64 * r + 2 * (2 * n + i) + upper, 3)
                yield 64 * upper, i, r, third, s


def build(nc, tok, table, wqk, wv, wo, wk2, wq2, wvT2, w2, r_w, r_b, fc_w, fc_b, pj_w, pj_b, ln, ln_cols, out):
    f32, bf16, i32, u32 = mybir.dt.float32, mybir.dt.bfloat16, mybir.dt.int32, mybir.dt.uint32
    ALU, ACT, AX = mybir.AluOpType, mybir.ActivationFunctionType, mybir.AxisListType
    nc.disable_value_cache = True
    HEAD = head_order()
    STRETCHES = stretches(HEAD, [(batch_order(True, False), 1), (batch_order(False, False), B - 2),
                                 (batch_order(False, True), 1), (tail_order(), 1)])
    HEAD_2 = channel_head()
    STRETCHES_2 = stretches(HEAD_2, [(channel_pair(False), B // 2 - 1), (channel_pair(True), 1)])

    whole = ExitStack()
    with whole:
        def keep(name, shape, dt):
            return whole.enter_context(nc.sbuf_tensor(name, shape, dt))
        hid = keep("hid", [P, B * TT, D], f32)
        ident = keep("ident", [P, P], f32)
        minus_half = keep("minus_half", [P, TT], f32)
        stat = keep("stat", [P, TT, nc.vector.BN_STATS_DIM], f32)
        mean_var = keep("mean_var", [P, TT, 2], f32)
        rstd = keep("rstd", [P, TT], f32)

        def run_stretches(eng, work, head, parts):
            work(head, Numbers({}, {}, 0), 0)
            run_batches(eng, work, parts)

        def run_batches(eng, work, parts):
            for batches, first, order, start in parts:
                if batches:
                    with eng.Fori(0, batches) as b:
                        work(order, Numbers(start, order.count, b, eng), b + first if first else b)
                else:
                    work(order, Numbers(start, {}, 0), first)

        def wait(eng, sem, value):
            if not isinstance(value, int) or value > 0:
                eng.wait_ge(sem, value)

        attn = ExitStack()
        with attn:
            def sb(name, shape, dt):
                return attn.enter_context(nc.sbuf_tensor(name, shape, dt))

            def pb(name, shape, dt=f32):
                return attn.enter_context(nc.psum_tensor(name, shape, dt))

            def sem(name):
                return attn.enter_context(nc.semaphore(name))

            ids = sb("ids", [P, B * TT], i32)
            wqk_sb = sb("wqk_sb", [KD, G, KT, P], f32)
            wv_sb = sb("wv_sb", [KD, KT, D], f32)
            wo_sb = sb("wo_sb", [P, G, D], f32)
            xT = sb("xT", [KD, KT, N], f32)
            part = [sb(f"part{i}", [P, 2, N], bf16) for i in range(3)]
            fresh = sb("fresh", [P, TT, D], f32)
            rest = sb("rest", [P, 2, HALF], f32)
            qs = sb("qs", [STACK + SHIFT, G, GROUP, N], bf16)
            ks = sb("ks", [STACK + SHIFT, G, GROUP, N], bf16)
            v_all = sb("v_all", [P, TT, D], f32)
            v = sb("v", [P, G, TT, GROUP, VW], f32)
            prob = sb("prob", [P, PROBS, GROUP, HALF], f32)
            maxima = sb("maxima", [P, TT, GROUP, NH], f32)
            negmax = sb("negmax", [P, TT, GROUP], f32)
            negpart = sb("negpart", [P, TT, SHIFT, GROUP], bf16)
            shift_row = sb("shift_row", [SHIFT * GROUP, HALF], bf16)
            mask = sb("mask", [P, HALF], bf16)
            identb = sb("identb", [P, P], bf16)
            pick = sb("pick", [P, GROUP], f32)
            rsum = sb("rsum", [P, 4 * GROUP], f32)
            rsum_b = sb("rsum_b", [P, 4, GROUP, 32], f32)
            on = sb("on", [P, G, N], f32)

            max_ps = pb("max_ps", [P, MAX_BANKS, HALF])
            score_ps = pb("score_ps", [P, 2, HALF])
            o_ps = pb("o_ps", [P, HALF])
            prep_ps = pb("prep_ps", [P, HALF])
            side_ps = pb("side_ps", [P, HALF])
            side_ps16 = side_ps[:, :].bitcast(bf16)

            ids_in = sem("ids_in")
            weights_in = sem("weights_in")
            gathered = [sem(f"gathered{b}") for b in range(B)]
            landed = sem("landed")
            const_pool = sem("const_pool")
            const_dve = sem("const_dve")
            stats_done = sem("stats_done")
            rstd_done = sem("rstd_done")
            ln_done = sem("ln_done")
            prep_filled = sem("prep_filled")
            prep_drained = sem("prep_drained")
            part1_done = sem("part1_done")
            part2_done = sem("part2_done")
            part3_done = sem("part3_done")
            stacked = sem("stacked")
            max_filled = sem("max_filled")
            max_drained = sem("max_drained")
            negated = sem("negated")
            side_filled = sem("side_filled")
            side_drained = sem("side_drained")
            sums_spread = sem("sums_spread")
            shifted = sem("shifted")
            score_filled = sem("score_filled")
            exp_done = sem("exp_done")
            masked = sem("masked")
            v_placed = sem("v_placed")
            value_done = sem("value_done")
            o_evacuated = sem("o_evacuated")

            STACK_DMAS = 16 * 2 * SLOTS
            SHIFT_DMAS = 16 * SHIFT
            block = attn.enter_context(nc.Block())

            passed = {eng: sem(f"passed_{name}") for name, eng in
                      (("vector", nc.vector), ("gpsimd", nc.gpsimd))}

            def run(eng, work):
                run_stretches(eng, work, HEAD, STRETCHES)

            def apart(eng):
                eng.sem_inc(passed[eng], 1)

            def prep_bank(order, w):
                other = order is HEAD and w["before"].get("prep", 0) % 2
                return score_ps[:, 1, :] if other else prep_ps[:, :]

            def half_of(w):
                return slice(HALF * w["half"], HALF * (w["half"] + 1))

            @block.sync
            def _(sp):
                sp.dma_start(ids[:, :], tok).then_inc(ids_in, 16)
                for dst, src in ((wqk_sb, wqk), (wv_sb, wv), (wo_sb, wo)):
                    sp.dma_start(dst[:], src).then_inc(weights_in, 16)
                sp.wait_ge(const_dve, 4)

                def work(order, before, b):
                    for kind, w in order.jobs:
                        if kind == "STACK":
                            wait(sp, stacked, before("STACK", w, STACK_DMAS))
                            sp.wait_ge(part3_done, before("QK", w))
                            for s in range(SLOTS):
                                for dst, which, row in ((qs, Q_PARTS[s], 0), (ks, K_PARTS[s], P // 2)):
                                    sp.dma_start(dst[DH * s:DH * (s + 1), w["g"], :, :],
                                                 part[which][row:row + P // 2, w["g"] % 2, :]).then_inc(stacked, 16)
                        if kind == "SHIFT":
                            sp.wait_ge(side_drained, before("side", w, 1, 2))
                            for r in range(SHIFT):
                                sp.dma_start(qs[STACK + r:STACK + r + 1, w["g"], :, half_of(w)],
                                             shift_row[GROUP * r:GROUP * (r + 1), :]).then_inc(shifted, 16)

                run(sp, work)

            @block.gpsimd
            def _(pool):
                def gather(tiles):
                    for i in tiles:
                        pool.indirect_dma_start(
                            out=hid[:, i, :], out_offset=None, in_=table,
                            in_offset=bass.IndirectOffsetOnAxis(ap=ids[:, i:i + 1].bitcast(u32), axis=0)
                        ).then_inc(gathered[i // TT], 16)

                def land(batches):
                    for b in batches:
                        pool.wait_ge(gathered[b], 16 * TT)
                        pool.sem_inc(landed, 1)

                pool.wait_ge(ids_in, 16)
                gather(range(TT))
                pool.memset(ident[:, :], 0.0).then_inc(const_pool, 1)
                pool.memset(identb[:, :], 0.0).then_inc(const_pool, 1)
                pool.memset(pick[:, :], 0.0).then_inc(const_pool, 1)
                pool.memset(mask[:, :], 0.0).then_inc(const_pool, 1)
                pool.memset(minus_half[:, :], -0.5).then_inc(const_pool, 1)
                pool.wait_ge(const_pool, 5)
                for m in (ident, identb):
                    pool.affine_select(out=m[:, :], in_=m[:, :], compare_op=ALU.not_equal, fill=1.0, base=0,
                                       pattern=[[-1, P]], channel_multiplier=1).then_inc(const_pool, 1)
                pool.affine_select(out=pick[:, :], in_=pick[:, :], compare_op=ALU.not_equal, fill=1.0, base=-DH,
                                   pattern=[[-32, GROUP]], channel_multiplier=1).then_inc(const_pool, 1)
                pool.affine_select(out=mask[:, HALF - P:HALF], in_=mask[:, HALF - P:HALF], compare_op=ALU.is_ge,
                                   fill=NEG, base=0, pattern=[[-1, P]], channel_multiplier=1).then_inc(const_pool, 1)

                def work(order, before, b):
                    for kind, w in order.jobs:
                        if kind == "RSTD":
                            pool.wait_ge(stats_done, before("RSTD", w, 2 * TT, 2 * TT))
                            apart(pool)
                            pool.tensor_scalar(rstd[:, :], mean_var[:, :, 1], LN_EPS, None, ALU.add).then_inc(rstd_done, 1)
                            pool.wait_ge(rstd_done, before("RSTD", w, 2, 1))
                            pool.tensor_tensor(rstd[:, :], rstd[:, :], minus_half[:, :], ALU.pow).then_inc(rstd_done, 1)
                        if kind == "VALUES":
                            pool.wait_ge(o_evacuated, before("UNIT", w, NH, 1))
                            pool.wait_ge(prep_drained, before("prep", w, 1, 1))
                            apart(pool)
                            pool.tensor_copy(v[:, w["g"], :, :, 0:DH],
                                             v_all[:, :, 64 * w["g"]:64 * (w["g"] + 1)].rearrange("p t (h d) -> p t h d", d=DH)
                                             ).then_inc(v_placed, 1)
                        if kind == "PART":
                            c = half_of(w)
                            pool.wait_ge(part2_done, before("PART", w, 1, 1))
                            pool.tensor_tensor(part[2][:, w["g"] % 2, c], rest[:, w["half"], :], part[1][:, w["g"] % 2, c], ALU.subtract).then_inc(part3_done, 1)
                        if kind == "SCORE" and diagonal(w["half"], w["kt"]) and w["h"] == GROUP - 1:
                            pool.wait_ge(exp_done, before("SCORE", w, 1, 3))
                            c = first_column(w["half"], w["kt"])
                            tile = prob[:, w["before"].get("BLOCK", 0) % PROBS, :, c:c + P]
                            apart(pool)
                            pool.affine_select(out=tile, in_=tile, compare_op=ALU.is_ge, fill=0.0, base=0,
                                               pattern=[[0, GROUP], [1, P]], channel_multiplier=-1).then_inc(masked, 1)
                            if order is STRETCHES[0][2]:
                                each = (B - 2) * TT // (G * TT)
                                at = 2 * TT + each * w["before"].get("DIAGONAL_SCORES", 0)
                                gather(range(at, at + each))
                    if order is STRETCHES[0][2]:
                        land(range(2, B))

                land([0])
                work(HEAD, Numbers({}, {}, 0), 0)
                gather(range(TT, 2 * TT))
                land([1])
                run_batches(pool, work, STRETCHES)

            @block.scalar
            def _(act):
                act.sem_inc(exp_done, 2)
                act.sem_inc(o_evacuated, 1)
                act.wait_ge(weights_in, 16 * 3)
                act.wait_ge(const_dve, 4)

                def work(order, before, b):
                    for kind, w in late(order.jobs, {"XT": 1, "QK": 1, "SHIFT": 1, "EVAC": 1}):
                        if kind == "XT":
                            act.wait_ge(prep_filled, before("prep", w, 1, 1))
                            act.activation(xT[:, w["k"], half_of(w)], prep_bank(order, w)[0:KD, :], ACT.Copy).then_inc(prep_drained, 1)
                        if kind == "QK":
                            wait(act, stacked, before("STACK", w, STACK_DMAS, -STACK_DMAS * (w["g"] % 2)))
                            act.wait_ge(prep_filled, before("prep", w, 1, 1))
                            act.activation(part[0][:, w["g"] % 2, half_of(w)], prep_bank(order, w), ACT.Copy).then_inc(part1_done, 1)
                        if kind == "PART":
                            act.wait_ge(prep_drained, before("prep", w, 1, 1))
                            act.activation(part[1][:, w["g"] % 2, half_of(w)], rest[:, w["half"], :], ACT.Copy).then_inc(part2_done, 1)
                        if kind == "SPREAD":
                            act.wait_ge(side_drained, before("side", w, 1, 1))
                            act.activation(rsum_b[:, :, :, :], rsum[:, :].rearrange("p (t h) -> p t h", h=GROUP)
                                           .unsqueeze(3).to_broadcast([P, 4, GROUP, 32]), ACT.Copy).then_inc(sums_spread, 1)
                        if kind == "SHIFT":
                            wait(act, shifted, before("SHIFT", w, SHIFT_DMAS))
                            act.wait_ge(side_filled, before("side", w, 1, 1))
                            act.activation(shift_row[:, :], side_ps16[0:SHIFT * GROUP, 0:HALF], ACT.Copy).then_inc(side_drained, 1)
                        if kind == "SCORE":
                            c = first_column(w["half"], w["kt"])
                            if w["h"] == 0:
                                act.wait_ge(value_done, before("BLOCK", w, 1, 1))
                            act.wait_ge(score_filled, before("SCORE", w, 1, 1))
                            act.activation(prob[:, w["before"].get("BLOCK", 0) % PROBS, w["h"], c:HALF],
                                           score_ps[:, w["before"].get("SCORE", 0) % 2, c:HALF],
                                           ACT.Exp, scale=SCORE_SCALE).then_inc(exp_done, 1)
                        if kind == "EVAC":
                            act.wait_ge(side_drained, before("side", w, 1, 1))
                            act.wait_ge(value_done, before("VALUE", w, 1, PROBS))
                            act.activation(on[:, w["g"], half_of(w)], o_ps[:, :], ACT.Copy).then_inc(o_evacuated, 1)

                run(act, work)

            @block.vector
            def _(dve):
                dve.memset(v[:, :, :, :, DH:VW], 1.0).then_inc(const_dve, 1)
                dve.memset(ks[STACK:STACK + SHIFT, :, :, :], 1.0).then_inc(const_dve, 1)
                dve.memset(o_ps[:, :], 0.0).then_inc(const_dve, 1)
                dve.memset(maxima[:, :, :, :], LOWEST).then_inc(const_dve, 1)
                dve.sem_inc(max_drained, MAX_BANKS)
                dve.sem_inc(side_drained, 1)
                dve.sem_inc(prep_drained, 1)
                dve.wait_ge(const_dve, 4)
                dve.wait_ge(const_pool, 9)
                dve.wait_ge(weights_in, 16 * 3)

                def row(x, i):
                    return x[:, bass.ds(i, 1), :].rearrange("p a d -> p (a d)")

                def work(order, before, b):
                    for kind, w in late(order.jobs, {"QK": 2, "V": 1, "SUMS": 1, "NORM": 1, "OUT": 1}):
                        nb = 0 if order is HEAD else b + 1
                        if kind == "STAT":
                            dve.wait_ge(landed, nb + 1)
                            for t in range(2 * w["i"], 2 * w["i"] + 2):
                                dve.bn_stats(stat[:, t, :], row(hid, TT * nb + t)).then_inc(stats_done, 1)
                            if w["i"] == 3:
                                dve.wait_ge(stats_done, before("RSTD", w, 2 * TT, TT))
                                apart(dve)
                                for t in range(TT):
                                    dve.bn_aggr(mean_var[:, t, :], stat[:, t, :]).then_inc(stats_done, 1)
                        if kind == "LN":
                            dve.wait_ge(rstd_done, before("LN", w, 2, 2))
                            for t in range(TT):
                                dve.tensor_scalar(fresh[:, t, :], row(hid, TT * nb + t), mean_var[:, t, 0:1],
                                                  rstd[:, t:t + 1], ALU.subtract, ALU.mult).then_inc(ln_done, 1)
                        if kind == "QK":
                            dve.wait_ge(part1_done, before("QK", w, 1, 1))
                            wait(dve, part3_done, before("QK", w, 1, -1))
                            dve.tensor_tensor(rest[:, w["half"], :], prep_bank(order, w), part[0][:, w["g"] % 2, half_of(w)],
                                              ALU.subtract).then_inc(prep_drained, 1)
                        if kind == "V":
                            dve.wait_ge(prep_filled, before("prep", w, 1, 1))
                            if w["pair"] == 0:
                                wait(dve, v_placed, before("VALUES", w))
                            dve.tensor_copy(v_all[:, 2 * w["pair"]:2 * w["pair"] + 2, :].rearrange("p t d -> p (t d)"),
                                            prep_bank(order, w)[:, 0:2 * D]).then_inc(prep_drained, 1)
                        if kind == "MAX":
                            dve.wait_ge(max_filled, before("MAX", w, 1, 1))
                            n = w["before"].get("MAX", 0)
                            to = maxima[:, w["t"], w["h"], w["c"]:w["c"] + 1]
                            if w["c"] == w["t"] // 4:
                                keys = P * (w["t"] % 4 + 1)
                                apart(dve)
                                dve.tensor_tensor_reduce(out=max_ps[:, n % MAX_BANKS, 0:keys], in0=max_ps[:, n % MAX_BANKS, 0:keys],
                                                         in1=mask[:, HALF - keys:HALF], scale=1.0, scalar=LOWEST,
                                                         op0=ALU.add, op1=ALU.max, accum_out=to).then_inc(max_drained, 1)
                            else:
                                dve.tensor_reduce(to, max_ps[:, n % MAX_BANKS, :], AX.X, ALU.max).then_inc(max_drained, 1)
                        if kind == "NEGATE":
                            ts = slice(4 * w["half"], 4 * w["half"] + 4)
                            seen = w["half"] + 1
                            dve.wait_ge(max_drained, before("MAX", w, 1, MAX_BANKS))
                            dve.tensor_reduce(negmax[:, ts, :], maxima[:, ts, :, 0:seen], AX.X, ALU.max,
                                              negate=True).then_inc(negated, 1)
                            dve.wait_ge(negated, before("NEGATE", w, 3, 1))
                            dve.tensor_copy(negpart[:, ts, 0, :], negmax[:, ts, :]).then_inc(negated, 1)
                            dve.wait_ge(negated, before("NEGATE", w, 3, 2))
                            dve.tensor_tensor(negpart[:, ts, 1, :], negmax[:, ts, :], negpart[:, ts, 0, :],
                                              ALU.subtract).then_inc(negated, 1)
                        if kind == "SUMS":
                            dve.wait_ge(side_filled, before("side", w, 1, 1))
                            dve.reciprocal(rsum[:, :], side_ps[:, 0:4 * GROUP]).then_inc(side_drained, 1)
                        if kind == "NORM":
                            dve.wait_ge(side_filled, before("side", w, 1, 1))
                            dve.tensor_tensor(on[:, w["g"], half_of(w)], on[:, w["g"], half_of(w)], side_ps[:, :],
                                              ALU.mult).then_inc(side_drained, 1)
                        if kind == "OUT":
                            dve.wait_ge(side_filled, before("side", w, 1, 1))
                            rows = hid[:, bass.ds(TT * (b - w["late"]) + 2 * w["pair"], 2), :]
                            dve.tensor_tensor(rows, side_ps[:, 0:2 * D].rearrange("p (t d) -> p t d", d=D), rows,
                                              ALU.add).then_inc(side_drained, 1)

                run(dve, work)

            @block.tensor
            def _(pe):
                pe.sem_inc(value_done, PROBS)
                pe.wait_ge(const_pool, 9)
                pe.wait_ge(const_dve, 4)
                pe.wait_ge(weights_in, 16 * 3)

                def transpose(out, in_, one):
                    return pe.matmul(out, in_, one, is_transpose=True, start=True, stop=True)

                def work(order, before, b):
                    for kind, w in order.jobs:
                        if kind in ("XT", "QK", "V"):
                            if kind == "XT" and w["k"] == 0 and w["half"] == 0:
                                pe.wait_ge(ln_done, before("LN", w, TT))
                            wait(pe, prep_drained, before("prep", w, 1, 0 if order is HEAD else 1))
                        if kind in ("SHIFT", "SUMS", "NORM", "OUT"):
                            pe.wait_ge(side_drained, before("side", w, 1, 1))
                        if kind == "XT":
                            for t in range(4):
                                ins = transpose(prep_bank(order, w)[0:KD, P * t:P * (t + 1)],
                                                fresh[:, 4 * w["half"] + t, KD * w["k"]:KD * (w["k"] + 1)], ident[:, :])
                            ins.then_inc(prep_filled, 1)
                        if kind == "QK":
                            for k in range(KT):
                                ins = pe.matmul(prep_bank(order, w), wqk_sb[:, w["g"], k, :],
                                                xT[:, k, half_of(w)], start=k == 0, stop=k == KT - 1)
                            ins.then_inc(prep_filled, 1)
                        if kind == "V":
                            for t in range(2):
                                first = P * (2 * w["pair"] + t)
                                for k in range(KT):
                                    ins = pe.matmul(prep_bank(order, w)[:, D * t:D * (t + 1)], xT[:, k, first:first + P],
                                                    wv_sb[:, k, :], start=k == 0, stop=k == KT - 1)
                            ins.then_inc(prep_filled, 1)
                        if kind == "MAX":
                            if w["t"] == 0 and w["h"] == 0 and w["c"] == 0:
                                pe.wait_ge(stacked, before("UNIT", w, STACK_DMAS, STACK_DMAS * (w["ahead"] + 1)))
                            pe.wait_ge(max_drained, before("MAX", w, 1, 1))
                            n = w["before"].get("MAX", 0)
                            keys = P * (w["t"] % 4 + 1) if w["c"] == w["t"] // 4 else HALF
                            pe.matmul(max_ps[:, n % MAX_BANKS, 0:keys], qs[0:STACK, w["g"], w["h"], P * w["t"]:P * (w["t"] + 1)],
                                      ks[0:STACK, w["g"], w["h"], HALF * w["c"]:HALF * w["c"] + keys],
                                      start=True, stop=True).then_inc(max_filled, 1)
                        if kind == "SHIFT":
                            pe.wait_ge(negated, before("SHIFT", w, 3, 3))
                            for t in range(4):
                                ins = transpose(side_ps16[0:SHIFT * GROUP, P * t:P * (t + 1)],
                                                negpart[:, 4 * w["half"] + t, :, :].rearrange("p s h -> p (s h)"), identb[:, :])
                            ins.then_inc(side_filled, 1)
                        if kind == "SCORE":
                            c = first_column(w["half"], w["kt"])
                            if w["kt"] == 0 and w["h"] == 0:
                                pe.wait_ge(shifted, before("UNIT", w, 2 * SHIFT_DMAS, (w["half"] + 1) * SHIFT_DMAS))
                            pe.wait_ge(exp_done, before("SCORE", w, 1, 1))
                            pe.matmul(score_ps[:, w["before"].get("SCORE", 0) % 2, c:HALF],
                                      ks[:, w["g"], w["h"], P * w["kt"]:P * (w["kt"] + 1)],
                                      qs[:, w["g"], w["h"], HALF * w["half"] + c:HALF * (w["half"] + 1)],
                                      start=True, stop=True).then_inc(score_filled, 1)
                        if kind == "VALUE":
                            c = first_column(w["half"], w["kt"])
                            if w["kt"] == 0:
                                if w["half"] == 0:
                                    pe.wait_ge(v_placed, before("UNIT", w, 1, 1))
                                pe.wait_ge(o_evacuated, before("EVAC", w, 1, 1))
                            pe.wait_ge(exp_done, before("VALUE", w, GROUP, GROUP + 2))
                            if diagonal(w["half"], w["kt"]):
                                pe.wait_ge(masked, before("DIAGONAL", w, 1, 1))
                            for h in range(GROUP):
                                ins = pe.matmul(o_ps[32 * h:32 * h + VW, c:HALF], v[:, w["g"], w["kt"], h, :],
                                                prob[:, w["before"].get("VALUE", 0) % PROBS, h, c:HALF],
                                                start=w["kt"] == 0, stop=w["last"])
                            ins.then_inc(value_done, 1)
                        if kind == "SUMS":
                            pe.wait_ge(o_evacuated, before("EVAC", w, 1, 1))
                            for t in range(4):
                                ins = pe.matmul(side_ps[:, GROUP * t:GROUP * (t + 1)], on[:, w["g"], HALF * w["half"] + P * t:HALF * w["half"] + P * (t + 1)],
                                                pick[:, :], start=True, stop=True)
                            ins.then_inc(side_filled, 1)
                        if kind == "NORM":
                            pe.wait_ge(sums_spread, before("NORM", w, 1, 1))
                            for t in range(4):
                                ins = transpose(side_ps[:, P * t:P * (t + 1)],
                                                rsum_b[:, t, :, :].rearrange("p h c -> p (h c)"), ident[:, :])
                            ins.then_inc(side_filled, 1)
                        if kind == "OUT":
                            for t in range(2):
                                i = 2 * w["pair"] + t
                                for g in range(G):
                                    ins = pe.matmul(side_ps[:, D * t:D * (t + 1)], on[:, g, P * i:P * (i + 1)],
                                                    wo_sb[:, g, :], start=g == 0, stop=g == G - 1)
                            ins.then_inc(side_filled, 1)

                run(pe, work)

        nrm = keep("nrm", [P, B * TT, D], f32)
        row_stats = keep("row_stats", [P, B * TT, nc.vector.BN_STATS_DIM], f32)
        act_h = keep("act_h", [P, TOP * FT, HALF], f32)
        y_sums = act_h[:, 0:B // 2, :].rearrange("p i n -> p (i n)")[:, 0:B * D].rearrange("p (b d) -> p b d", d=D)
        channel = ExitStack()
        with channel:
            def sb(name, shape, dt=f32):
                return channel.enter_context(nc.sbuf_tensor(name, shape, dt))

            def pb(name, shape):
                return channel.enter_context(nc.psum_tensor(name, shape, f32))

            def sem(name):
                return channel.enter_context(nc.semaphore(name))

            wq_sb = sb("wq2_sb", [KD + 1, KT, D])
            wk_sb = sb("wk2_sb", [KD + 1, KT, D])
            wvT_sb = sb("wvT2_sb", [KD, KT, D + 1])
            w2_sb = sb("w2_sb", [P, 2, D])
            x = sb("x_rows", [P, TT, D + 1])
            xT = sb("xT2", [KD + 1, 2, KT, N])
            gram = sb("gram", [KD + 1, KT, D + 1])
            mixed = sb("mixed", [KD + 1, KT, D])
            blocks = sb("blocks", [KD, KT, KD])
            s_masked = sb("s_masked", [KD, KT, KD])
            s_top = sb("s_top", [KD, KT])
            s_low = sb("s_low", [KD, KT, KD])
            s_exp = sb("s_exp", [KD, KT, KD])
            s_sum = sb("s_sum", [KD, KT])
            s_inv = sb("s_inv", [KD, KT])
            attend = sb("attend", [KD, KT, KD])
            attendT = sb("attendT", [KD, KT, KD])
            united = sb("united", [KD + 1, KT, D])
            rowsT = sb("rowsT", [P, 2, 64, 16])
            fold_4 = sb("fold_4", [P, 4, D])
            fold_2 = sb("fold_2", [P, 2, D])
            xt_ps = pb("xt2_ps", [P, 2, HALF])
            gram_ps = pb("gram_ps", [P, HALF])
            chain_ps = pb("chain_ps", [P, HALF])
            rows_ps = pb("rows_ps", [P, 2, HALF])
            out_ps = pb("out_ps", [P, 2, HALF])

            weights_in = sem("weights2_in")
            const_pool = sem("const2_pool")
            const_dve = sem("const2_dve")
            stats_done = sem("stats2a_done")
            rstd_done = sem("rstd2_done")
            ln_done = sem("ln2_done")
            kept = sem("kept")
            turned = sem("turned")
            turned_out = sem("turned_out")
            gram_filled = sem("gram_filled")
            gram_out = sem("gram_out")
            chain_filled = sem("chain_filled")
            chain_out = sem("chain_out")
            low_done = sem("low_done")
            exp2_done = sem("exp2_done")
            soft = sem("soft")
            rows_filled = sem("rows_filled")
            rows_out_act = sem("rows_out_act")
            rows_out_dve = sem("rows_out_dve")
            out_filled = sem("out_filled")
            out_out = sem("out_out")
            out_stats = sem("out_stats")
            folded = sem("folded")
            passed = {eng: sem(f"passed2_{name}") for name, eng in (("vector", nc.vector), ("gpsimd", nc.gpsimd))}
            block = channel.enter_context(nc.Block())

            def apart(eng):
                eng.sem_inc(passed[eng], 1)

            def run(eng, work):
                run_stretches(eng, work, HEAD_2, STRETCHES_2)

            def tiles(b, w, t=0):
                return b * (2 * TT) + (TT * w["u"] + t)

            def outputs_of(w, first, i, r):
                return rows_ps[first:first + THIRD, w["n"] % 2, D * i:D * (i + 1)].rearrange("p (q r) -> p r q", r=3)[:, r, :]

            def third_of(third):
                first = THIRD * (third % 2)
                return rowsT[first:first + THIRD, third // 2, :, :]

            @block.sync
            def _(sp):
                for dst, src in ((wq_sb, wq2), (wk_sb, wk2), (wvT_sb, wvT2), (w2_sb, w2)):
                    sp.dma_start(dst[:, :, :], src).then_inc(weights_in, 16)

            @block.gpsimd
            def _(pool):
                pool.memset(blocks[:, :, :], 0.0).then_inc(const_pool, 1)
                pool.wait_ge(const_pool, 1)
                heads = blocks[:, :, :].rearrange("p k (h d) -> p k h d", d=DH)
                pool.affine_select(out=heads, in_=heads, compare_op=ALU.is_ge, fill=NEG, base=0,
                                   pattern=[[0, KT], [-DH, KD // DH], [0, DH]], channel_multiplier=1).then_inc(const_pool, 1)
                pool.wait_ge(const_pool, 2)
                pool.affine_select(out=heads, in_=heads, compare_op=ALU.is_ge, fill=NEG, base=DH - 1,
                                   pattern=[[0, KT], [DH, KD // DH], [0, DH]], channel_multiplier=-1).then_inc(const_pool, 1)

                def work(order, before, b):
                    for kind, w in order.jobs:
                        if kind == "STAT":
                            pool.wait_ge(stats_done, before("STAT", w, 2 * TT, 2 * TT))
                            apart(pool)
                            pool.tensor_scalar(rstd[:, :], mean_var[:, :, 1], LN_EPS, None, ALU.add).then_inc(rstd_done, 1)
                            pool.wait_ge(rstd_done, before("STAT", w, 2, 1))
                            pool.tensor_tensor(rstd[:, :], rstd[:, :], minus_half[:, :], ALU.pow).then_inc(rstd_done, 1)
                            if order is HEAD_2 and w["u"] == 0:
                                pool.wait_ge(rstd_done, 2)
                                pool.memset(xT[KD:KD + 1, :, :, :], 1.0).then_inc(const_pool, 1)
                                pool.wait_ge(const_pool, 4)
                                pool.memset(rowsT[THIRD:THIRD + 1, 1, :, :], 1.0).then_inc(const_pool, 1)
                                pool.wait_ge(const_pool, 5)
                        if kind == "LN":
                            pool.wait_ge(ln_done, before("LN", w, TT, TT))
                            apart(pool)
                            pool.tensor_copy(nrm[:, bass.ds(tiles(b, w), TT), :], x[:, :, 0:D]).then_inc(kept, 1)
                        if kind == "FOLD":
                            pool.wait_ge(out_out, before("OUT", w, 1, 2))
                            pool.tensor_tensor(fold_4[:, :, :], nrm[:, bass.ds(tiles(b, w), 4), :],
                                               nrm[:, bass.ds(tiles(b, w, 4), 4), :], ALU.add).then_inc(folded, 1)
                            pool.wait_ge(folded, before("FOLD", w, 3, 1))
                            pool.tensor_tensor(fold_2[:, :, :], fold_4[:, 0:2, :], fold_4[:, 2:4, :], ALU.add).then_inc(folded, 1)
                            pool.wait_ge(folded, before("FOLD", w, 3, 2))
                            pool.tensor_tensor(y_sums[:, bass.ds(b * 2 + w["u"], 1), :].rearrange("p a d -> p (a d)"),
                                               fold_2[:, 0, :], fold_2[:, 1, :], ALU.add).then_inc(folded, 1)

                run(pool, work)

            @block.scalar
            def _(act):
                act.sem_inc(turned_out, 2)
                act.sem_inc(gram_out, 1)
                act.sem_inc(rows_out_act, 2)

                def work(order, before, b):
                    for kind, w in order.jobs:
                        if kind == "XT":
                            act.wait_ge(turned, before("XT", w, 1, 1))
                            act.activation(xT[0:KD, w["u"], w["k"], HALF * w["half"]:HALF * (w["half"] + 1)],
                                           xt_ps[0:KD, w["half"], :], ACT.Copy).then_inc(turned_out, 1)
                        if kind == "GRAM":
                            act.wait_ge(gram_filled, before("GRAM", w, 1, 1))
                            act.activation(gram[0:TALL[w["i"]], w["i"], :], gram_ps[0:TALL[w["i"]], 0:D + 1],
                                           ACT.Copy).then_inc(gram_out, 1)
                        if kind == "SCORES":
                            act.wait_ge(low_done, before("SCORES", w, 1, 1))
                            act.activation(s_exp[:, :, :], s_low[:, :, :], ACT.Exp, scale=CHANNEL_SCALE).then_inc(exp2_done, 1)
                        if kind == "ROWS":
                            act.wait_ge(rows_filled, before("ROWS", w, 1, 1))
                            for first, i, r, third, srow in rows_of(w["n"]):
                                if first:
                                    ins = act.activation(third_of(third)[:, :, srow], outputs_of(w, first, i, r), ACT.Copy)
                            ins.then_inc(rows_out_act, 1)

                run(act, work)

            @block.vector
            def _(dve):
                dve.memset(x[:, :, D:D + 1], 1.0).then_inc(const_dve, 1)
                dve.sem_inc(chain_out, 1)
                dve.sem_inc(out_out, 2)
                dve.sem_inc(rows_out_dve, 2)

                def row(t, i):
                    return t[:, bass.ds(i, 1), :].rearrange("p a d -> p (a d)")

                def work(order, before, b):
                    for kind, w in order.jobs:
                        if kind == "STAT":
                            for t in range(TT):
                                dve.bn_stats(stat[:, t, :], row(hid, tiles(b, w, t))).then_inc(stats_done, 1)
                            dve.wait_ge(stats_done, before("STAT", w, 2 * TT, TT))
                            apart(dve)
                            for t in range(TT):
                                dve.bn_aggr(mean_var[:, t, :], stat[:, t, :]).then_inc(stats_done, 1)
                        if kind == "LN":
                            wait(dve, turned, before("XT", w))
                            wait(dve, kept, before("LN", w))
                            dve.wait_ge(rstd_done, before("LN", w, 2, 2))
                            for t in range(TT):
                                dve.tensor_scalar(x[:, t, 0:D], row(hid, tiles(b, w, t)), mean_var[:, t, 0:1],
                                                  rstd[:, t:t + 1], ALU.subtract, ALU.mult).then_inc(ln_done, 1)
                        if kind == "MIX":
                            dve.wait_ge(chain_filled, before("MIX", w, 4, 1))
                            for k in range(KT):
                                ins = dve.tensor_copy(mixed[0:TALL[k], k, :], chain_ps[0:TALL[k], D * k:D * (k + 1)])
                            ins.then_inc(chain_out, 1)
                        if kind == "SCORES":
                            dve.wait_ge(chain_filled, before("SCORES", w, 4, 2))
                            dve.wait_ge(const_pool, 3)
                            apart(dve)
                            s_ps = chain_ps[0:KD, 0:D].rearrange("p (m e) -> p m e", m=KT)
                            dve.tensor_tensor(s_masked[:, :, :], s_ps, blocks[:, :, :], ALU.add).then_inc(chain_out, 1)
                            dve.wait_ge(chain_out, before("SCORES", w, 4, 3))
                            dve.tensor_reduce(s_top[:, :], s_masked[:, :, :], AX.X, ALU.max).then_inc(soft, 1)
                            dve.wait_ge(soft, before("SCORES", w, 4, 1))
                            dve.tensor_tensor(s_low[:, :, :], s_masked[:, :, :], s_top[:, :].unsqueeze(2).to_broadcast([KD, KT, KD]),
                                              ALU.subtract).then_inc(low_done, 1)
                            dve.wait_ge(exp2_done, before("SCORES", w, 1, 1))
                            dve.tensor_reduce(s_sum[:, :], s_exp[:, :, :], AX.X, ALU.add).then_inc(soft, 1)
                            dve.wait_ge(soft, before("SCORES", w, 4, 2))
                            dve.reciprocal(s_inv[:, :], s_sum[:, :]).then_inc(soft, 1)
                            dve.wait_ge(soft, before("SCORES", w, 4, 3))
                            dve.tensor_tensor(attend[:, :, :], s_exp[:, :, :], s_inv[:, :].unsqueeze(2).to_broadcast([KD, KT, KD]),
                                              ALU.mult).then_inc(soft, 1)
                        if kind == "TURN":
                            dve.wait_ge(chain_filled, before("TURN", w, 4, 3))
                            dve.tensor_copy(attendT[:, :, :], chain_ps[0:KD, 0:D].rearrange("p (m c) -> p m c", m=KT)).then_inc(chain_out, 1)
                        if kind == "UNITE":
                            dve.wait_ge(chain_filled, before("UNITE", w, 4, 4))
                            for k in range(KT):
                                ins = dve.tensor_copy(united[0:TALL[k], k, :], chain_ps[0:TALL[k], D * k:D * (k + 1)])
                            ins.then_inc(chain_out, 1)
                        if kind == "ROWS":
                            dve.wait_ge(rows_filled, before("ROWS", w, 1, 1))
                            apart(dve)
                            for first, i, r, third, srow in rows_of(w["n"]):
                                if not first:
                                    ins = dve.tensor_copy(third_of(third)[:, :, srow], outputs_of(w, first, i, r))
                            ins.then_inc(rows_out_dve, 1)
                        if kind == "OUT":
                            if w["pair"] == 0:
                                dve.wait_ge(kept, before("MIX", w))
                            dve.wait_ge(out_filled, before("OUT", w, 1, 1))
                            rows = nrm[:, bass.ds(tiles(b, w, 2 * w["pair"]), 2), :]
                            dve.tensor_tensor(rows, out_ps[:, w["pair"] % 2, 0:2 * D].rearrange("p (t d) -> p t d", d=D), rows,
                                              ALU.add).then_inc(out_out, 1)
                            dve.wait_ge(out_out, before("OUT", w, 1, 3))
                            for t in range(2):
                                dve.bn_stats(row(row_stats, tiles(b, w, 2 * w["pair"] + t)),
                                             row(nrm, tiles(b, w, 2 * w["pair"] + t))).then_inc(out_stats, 1)

                run(dve, work)
                dve.wait_ge(out_stats, B * TT)

            @block.tensor
            def _(pe):
                pe.wait_ge(const_dve, 1)

                def transpose(out, in_, one):
                    return pe.matmul(out, in_, one, is_transpose=True, start=True, stop=True)

                def tile(k):
                    return slice(KD * k, KD * k + TALL[k])

                def work(order, before, b):
                    for kind, w in order.jobs:
                        if kind == "GRAM":
                            if w["i"] == 0:
                                pe.wait_ge(ln_done, before("GRAM", w, TT // 2, TT))
                            pe.wait_ge(gram_out, before("GRAM", w, 1, 1))
                            for t in range(TT):
                                ins = pe.matmul(gram_ps[0:TALL[w["i"]], 0:D + 1], x[:, t, tile(w["i"])], x[:, t, :],
                                                start=t == 0, stop=t == TT - 1)
                            ins.then_inc(gram_filled, 1)
                        if kind == "XT":
                            pe.wait_ge(turned_out, before("XT", w, 1, 1))
                            for t in range(4):
                                ins = transpose(xt_ps[0:KD, w["half"], P * t:P * (t + 1)],
                                                x[:, 4 * w["half"] + t, KD * w["k"]:KD * (w["k"] + 1)], ident[:, :])
                            ins.then_inc(turned, 1)
                        if kind == "MIX":
                            pe.wait_ge(gram_out, before("MIX", w, KT, KT + 1))
                            pe.wait_ge(weights_in, 16 * 4)
                            pe.wait_ge(chain_out, before("MIX", w, 4, 1))
                            for i in range(KT):
                                for k in range(KT):
                                    ins = pe.matmul(chain_ps[0:TALL[i], D * i:D * (i + 1)], gram[0:TALL[k], k, tile(i)],
                                                    wk_sb[0:TALL[k], k, :], start=k == 0, stop=k == KT - 1)
                            ins.then_inc(chain_filled, 1)
                        if kind == "SCORES":
                            pe.wait_ge(chain_out, before("SCORES", w, 4, 2))
                            for m in range(KT):
                                for k in range(KT):
                                    ins = pe.matmul(chain_ps[0:KD, KD * m:KD * (m + 1)], wq_sb[0:TALL[k], k, KD * m:KD * (m + 1)],
                                                    mixed[0:TALL[k], k, KD * m:KD * (m + 1)], start=k == 0, stop=k == KT - 1)
                            ins.then_inc(chain_filled, 1)
                        if kind == "TURN":
                            pe.wait_ge(soft, before("TURN", w, 4, 4))
                            pe.wait_ge(chain_out, before("TURN", w, 4, 3))
                            for m in range(KT):
                                ins = transpose(chain_ps[0:KD, KD * m:KD * (m + 1)], attend[:, m, :], ident[0:KD, 0:KD])
                            ins.then_inc(chain_filled, 1)
                        if kind == "UNITE":
                            pe.wait_ge(chain_out, before("UNITE", w, 4, 4))
                            for k in range(KT):
                                for m in range(KT):
                                    ins = pe.matmul(chain_ps[0:TALL[k], D * k + KD * m:D * k + KD * (m + 1)],
                                                    wvT_sb[:, m, tile(k)], attendT[:, m, :], start=True, stop=True)
                            ins.then_inc(chain_filled, 1)
                        if kind == "ROWS":
                            if w["n"] == 0:
                                pe.wait_ge(const_pool, 5)
                                pe.wait_ge(chain_out, before("UNITE", w, 4, 1))
                                pe.wait_ge(turned_out, before("UNITE", w, 4, 2))
                            pe.wait_ge(rows_out_act, before("ROWS", w, 1, 1))
                            pe.wait_ge(rows_out_dve, before("ROWS", w, 1, 1))
                            for i in range(2):
                                first = P * (2 * w["n"] + i)
                                for k in range(KT):
                                    ins = pe.matmul(rows_ps[:, w["n"] % 2, D * i:D * (i + 1)], xT[0:TALL[k], w["u"], k, first:first + P],
                                                    united[0:TALL[k], k, :], start=k == 0, stop=k == KT - 1)
                            ins.then_inc(rows_filled, 1)
                        if kind == "OUT":
                            if w["pair"] == 0:
                                pe.wait_ge(rows_out_act, before("ROWS", w, 1, 2))
                                pe.wait_ge(rows_out_dve, before("ROWS", w, 1, 2))
                            pe.wait_ge(out_out, before("OUT", w, 1, 1))
                            for t in range(2):
                                for a, depth in ((0, P), (1, THIRD + 1)):
                                    cols = rowsT[0:depth, a, 8 * (2 * w["pair"] + t):8 * (2 * w["pair"] + t + 1), :]
                                    ins = pe.matmul(out_ps[:, w["pair"] % 2, D * t:D * (t + 1)], cols.rearrange("p q s -> p (q s)"),
                                                    w2_sb[0:depth, a, :], start=a == 0, stop=a == KT - 1)
                            ins.then_inc(out_filled, 1)

                run(pe, work)

        moe = ExitStack()
        with moe:
            def sb(name, shape, dt=f32):
                return moe.enter_context(nc.sbuf_tensor(name, shape, dt))

            def pb(name, shape):
                return moe.enter_context(nc.psum_tensor(name, shape, f32))

            def sem(name):
                return moe.enter_context(nc.semaphore(name))

            ROWS = B * TT
            BY_DVE = (5, 6, 7)
            LAST_ORDER = (0, 1, 5, 2, 6, 3, 7, 4)
            WRITE_ORDER = (0, 5, 1, 6, 2, 3, 7, 4)
            stats = row_stats
            COUNT = B * N * D
            HT = TOP * FT
            split = mybir.dt.float32r
            fc_raw = sb("fc_raw", [P, TOP, 2, F])
            fc_high = sb("fc_high", [P, TOP, 2, F], split)
            fc_low = sb("fc_low", [P, TOP, 2, F], split)
            pj = sb("pj", [P, 2, TOP, FT, D])
            fcb = sb("fcb", [P, 2, TOP, FT])
            pjb = sb("pjb", [P, 2, TOP, D])
            pj_bias = sb("pj_bias", [P, 2, D])
            bias_0 = sb("bias_0", [P, D])
            x1 = sb("x1", [P, TT, D])
            x1T = sb("x1T", [P, 3, N], split)
            ln_b = sb("ln_b", [P, 4, D])
            ln_f = sb("ln_f", [KD, 2, KT])
            rw = sb("rw", [KD, KT, E])
            rb = sb("rb", [B, E])
            moments = sb("moments", [P, 2, 2])
            overall = sb("overall", [P, 2, 8])
            spread = sb("spread", [P, 2, 2])
            average = sb("average", [P, P])
            one_row = sb("one_row", [1, P])
            a_b = sb("a_b", [P, D])
            c_b = sb("c_b", [P, D])
            a_f = sb("a_f", [KD, KT])
            a_n = sb("a_n", [KD, KT])
            c_f = sb("c_f", [KD, KT])
            xmean = sb("xmean", [KD, KT, B])
            logits = sb("logits", [B, E])
            negtop = sb("negtop", [B, 1])
            expo = sb("expo", [B, E])
            total = sb("total", [B, 1])
            rtotal = sb("rtotal", [B, 1])
            gate = sb("gate", [B, E])
            best = sb("best", [B, E])
            which = sb("which", [B, E], u32)
            best_row = sb("best_row", [1, B * TOP])
            which_row = sb("which_row", [1, B * TOP], u32)
            gates = sb("gates", [P, B * TOP])

            fc_ps = pb("fc_ps", [P, 4, HALF])
            z_ps = pb("z_ps", [P, 2, HALF])
            xt_ps = pb("xt_ps", [P, 2, HALF])

            consts_in = sem("consts_in")
            const_done = sem("const_done")
            fc_in = [sem("fc_in_even"), sem("fc_in_odd")]
            pj_in = [sem("pj_in_even"), sem("pj_in_odd")]
            small = sem("small")
            small_pe = sem("small_pe")
            small_pool = sem("small_pool")
            small_act = sem("small_act")
            rows_in = sem("rows_in")
            scaled = sem("scaled")
            x1_half = sem("x1_half")
            x1_done = sem("x1_done")
            bias_half = sem("bias_half")
            bias_done = sem("bias_done")
            x1_kept = sem("x1_kept")
            xt_filled = sem("xt_filled")
            xt_high = sem("xt_high")
            xt_drained = sem("xt_drained")
            fc_high_done = sem("fc_high_done")
            fc_low_done = sem("fc_low_done")
            fc_filled = sem("fc_filled")
            gelu_done = sem("gelu_done")
            z_filled = sem("z_filled")
            z_drained = sem("z_drained")
            stats2_done = sem("stats2_done")
            finished = sem("finished")
            final_1 = sem("final_1")
            final_2 = sem("final_2")
            final_3 = sem("final_3")
            written = sem("written")
            passed = sem("passed")
            passed_pe = sem("passed_pe")

            FC_LOADS, PJ_LOADS = 16 * 4 * TOP, 16 * 2 * TOP
            block = moe.enter_context(nc.Block())

            class Batch:

                def __init__(self, pair, odd):
                    self.pair, self.odd = pair, odd

                def times(self, each, more=0):
                    return self.pair * (2 * each) + (self.odd * each + more)

            def by_batch(eng, work):
                with eng.Fori(0, B // 2 - 1) as pair:
                    for odd in range(2):
                        work(Batch(pair, odd), True)
                for odd in range(2):
                    work(Batch(B // 2 - 1, odd), odd == 0)

            def high_x(k, half):
                return x1T[0:(P, THIRD)[k], 2 * k, HALF * half:HALF * (half + 1)]

            def low_x(k, half):
                return x1T[(0, THIRD)[k]:P, k + 1, HALF * half:HALF * (half + 1)]

            def turned_x(k, half):
                return xt_ps[0:(P, THIRD)[k], half, :]

            @block.sync
            def _(sp):
                for i in range(4):
                    sp.dma_start(ln_b[:, i, :], ln[i].partition_broadcast(P)).then_inc(consts_in, 16)
                sp.dma_start(ln_f[:, :, :], ln_cols).then_inc(consts_in, 16)
                sp.dma_start(rw[:, :, :], r_w.rearrange("(k p) e -> p k e", p=KD)).then_inc(consts_in, 16)
                sp.dma_start(rb[:, :], r_b.partition_broadcast(B)).then_inc(consts_in, 16)
                sp.wait_ge(small, CHOSEN)
                sp.dma_start(best_row[:, :], best[:, 0:TOP]).then_inc(rows_in, 16)
                sp.dma_start(which_row[:, :], which[:, 0:TOP]).then_inc(rows_in, 16)
                sp.wait_ge(rows_in, 32)

                def load(batch, parity):
                    chosen = [sp.value_load(which_row[0:1, bass.ds(batch.times(TOP, c), 1)], min_val=0, max_val=E - 1)
                              for c in range(TOP)]
                    for c, e in enumerate(chosen):
                        for rows, k, features in ((slice(0, P), 0, slice(0, P)), (slice(0, THIRD), 1, slice(P, D)),
                                                  (slice(THIRD, P), 1, slice(P, D))):
                            sp.dma_start(fc_raw[rows, c, k, :], fc_w[bass.ds(e, 1), features, :].rearrange("a p f -> p (a f)")).then_inc(fc_in[parity], 16)
                        sp.dma_start(fcb[:, parity, c, :], fc_b[bass.ds(e, 1), :, :].rearrange("a p t -> p (a t)")).then_inc(fc_in[parity], 16)
                    for c, e in enumerate(chosen):
                        sp.dma_start(pj[:, parity, c, :, :], pj_w[bass.ds(e, 1), :, :].rearrange("a (t p) d -> p (a t) d", p=P)).then_inc(pj_in[parity], 16)
                        sp.dma_start(pjb[:, parity, c, :], pj_b[bass.ds(e, 1), :].rearrange("a d -> (a d)").partition_broadcast(P)).then_inc(pj_in[parity], 16)

                def work(batch, more):
                    if more:
                        sp.wait_ge(bias_done, batch.times(1, 1))
                        sp.sem_inc(passed, 1)
                        nxt = Batch(batch.pair, 1) if batch.odd == 0 else Batch(batch.pair + 1, 0)
                        load(nxt, 1 - batch.odd)

                load(Batch(0, 0), 0)
                by_batch(sp, work)
                for i, b in enumerate(WRITE_ORDER):
                    by_dve = sum(c in BY_DVE for c in WRITE_ORDER[:i + 1])
                    if b in BY_DVE:
                        sp.wait_ge(final_3, by_dve)
                    else:
                        sp.wait_ge(final_2, i + 1 - by_dve)
                    sp.dma_start(out[b].rearrange("(t p) d -> p t d", p=P), nrm[:, TT * b:TT * (b + 1), :]).then_inc(written, 16)
                sp.wait_ge(written, 16 * B)

            @block.gpsimd
            def _(pool):
                pool.memset(average[:, :], 1.0 / P).then_inc(const_done, 1)
                pool.memset(one_row[:, :], 1.0).then_inc(const_done, 1)

                def inverse_root(norm):
                    pool.tensor_tensor(overall[:, norm, 4:5], overall[:, norm, 3:4], minus_half[:, 0:1], ALU.pow).then_inc(small_pool, 1)

                pool.wait_ge(small, VARIANCE)
                inverse_root(0)

                def work(batch, more):
                    pool.wait_ge(x1_done, batch.times(1, 1))
                    pool.wait_ge(bias_done, batch.times(1, 1))
                    pool.tensor_tensor(nrm[:, bass.ds(batch.times(TT), TT), :], x1[:, :, :],
                                       pj_bias[:, batch.odd, :].unsqueeze(1).to_broadcast([P, TT, D]), ALU.add).then_inc(x1_kept, 1)
                    rows = hid[:, bass.ds(batch.times(TT), TT), :]
                    pool.tensor_tensor(rows, rows, ln_b[:, 3, :].unsqueeze(1).to_broadcast([P, TT, D]), ALU.add).then_inc(finished, 1)
                    pool.wait_ge(stats2_done, batch.times(TT, TT))
                    rows = nrm[:, bass.ds(batch.times(TT), TT), :]
                    pool.tensor_tensor(rows, rows, ln_b[:, 2, :].unsqueeze(1).to_broadcast([P, TT, D]), ALU.mult).then_inc(finished, 1)

                pool.wait_ge(consts_in, 16 * 7)
                by_batch(pool, work)
                pool.wait_ge(small, VARIANCE_2)
                inverse_root(1)
                pool.wait_ge(small, ADDEND)
                for i, b in enumerate(LAST_ORDER):
                    if b in BY_DVE:
                        continue
                    pool.wait_ge(final_1, i + 1)
                    rows = nrm[:, TT * b:TT * (b + 1), :]
                    pool.tensor_tensor(rows, rows, c_b[:, :].unsqueeze(1).to_broadcast([P, TT, D]), ALU.add).then_inc(final_2, 1)

            @block.scalar
            def _(act):
                act.sem_inc(gelu_done, 4)
                act.wait_ge(small, NEGTOP)
                act.activation(expo[:, :], logits[:, :], ACT.Exp, bias=negtop[:, 0:1], accum_out=total[:, 0:1]).then_inc(small_act, 1)

                def turn(first):
                    for k in range(2):
                        for half in range(NH):
                            act.wait_ge(xt_filled, first + (NH * k + half + 1))
                            act.activation(high_x(k, half), turned_x(k, half), ACT.Copy).then_inc(xt_high, 1)

                def split_high(pair, parity):
                    act.wait_ge(fc_in[parity], pair * FC_LOADS + FC_LOADS)
                    for c in range(TOP):
                        act.activation(fc_high[:, c, :, :], fc_raw[:, c, :, :], ACT.Copy).then_inc(fc_high_done, 1)

                def work(batch, more):
                    for half in range(NH):
                        for i in range(HT):
                            act.wait_ge(fc_filled, batch.times(NH * HT, HT * half + i + 1))
                            act.activation(act_h[:, i, :], fc_ps[:, i % 4, :], ACT.Gelu_apprx_tanh,
                                           bias=fcb[:, batch.odd, i // FT, i % FT:i % FT + 1]).then_inc(gelu_done, 1)
                    if more:
                        turn(batch.times(4, 4))
                        split_high(batch.pair + batch.odd, 1 - batch.odd)

                turn(0)
                split_high(0, 0)
                by_batch(act, work)

            count = [0]

            @block.vector
            def _(dve):
                dve.sem_inc(z_drained, 2)
                dve.sem_inc(xt_drained, 2)

                def mark(ins, name=None):
                    ins.then_inc(small, 1)
                    count[0] += 1
                    dve.wait_ge(small, count[0])
                    if name:
                        assert count[0] == name, (count[0], name)

                def global_norm(norm, pe_at, variance, negmean):
                    o = overall[:, norm, :]
                    mark(dve.bn_aggr(moments[:, norm, :], stats[:, :, :].rearrange("p r s -> p (r s)")))
                    dve.wait_ge(small_pe, pe_at)
                    mark(dve.tensor_copy(o[:, 0:2], xt_ps[:, norm, 0:2]))
                    mark(dve.tensor_tensor(spread[:, norm, 0:1], moments[:, norm, 0:1], o[:, 0:1], ALU.subtract))
                    mark(dve.tensor_tensor(spread[:, norm, 1:2], spread[:, norm, 0:1], spread[:, norm, 0:1], ALU.mult))
                    dve.wait_ge(small_pe, pe_at + 1)
                    mark(dve.tensor_tensor(o[:, 2:3], xt_ps[:, norm, 4:5], o[:, 1:2], ALU.add))
                    mark(dve.tensor_scalar(o[:, 3:4], o[:, 2:3], COUNT / (COUNT - 1.0), GLOBAL_EPS, ALU.mult, ALU.add), variance)
                    mark(dve.tensor_scalar(o[:, 5:6], o[:, 0:1], -1.0, None, ALU.mult), negmean)
                    dve.wait_ge(small_pool, norm + 1)

                global_norm(0, 1, VARIANCE, VARIANCE + 1)
                dve.wait_ge(consts_in, 16 * 7)
                o = overall[:, 0, :]
                mark(dve.tensor_scalar(a_b[:, :], ln_b[:, 0, :], o[:, 4:5], None, ALU.mult))
                mark(dve.scalar_tensor_tensor(c_b[:, :], a_b[:, :], o[:, 5:6], ln_b[:, 1, :], ALU.mult, ALU.add))
                mark(dve.tensor_scalar(a_f[:, :], ln_f[:, 0, :], o[0:KD, 4:5], None, ALU.mult))
                mark(dve.scalar_tensor_tensor(c_f[:, :], a_f[:, :], o[0:KD, 5:6], ln_f[:, 1, :], ALU.mult, ALU.add))
                mark(dve.tensor_scalar(a_n[:, :], a_f[:, :], P / N, None, ALU.mult))
                dve.wait_ge(small_pe, 3)
                for k in range(KT):
                    mark(dve.tensor_scalar(xmean[:, k, :], fc_ps[0:KD, 1, B * k:B * (k + 1)], a_n[:, k:k + 1], c_f[:, k:k + 1],
                                           ALU.mult, ALU.add), XMEAN - KT + 1 + k)
                dve.wait_ge(small_pe, 4)
                mark(dve.tensor_tensor(logits[:, :], fc_ps[0:B, 2, 0:E], rb[:, :], ALU.add))
                mark(dve.tensor_reduce(negtop[:, 0:1], logits[:, :], AX.X, ALU.max, negate=True), NEGTOP)
                dve.wait_ge(small_act, 1)
                mark(dve.reciprocal(rtotal[:, :], total[:, :]))
                mark(dve.tensor_scalar(gate[:, :], expo[:, :], rtotal[:, 0:1], None, ALU.mult))
                mark(dve.max(best[:, :], gate[:, :]))
                mark(dve.max_index(which[:, :], best[:, :], gate[:, :]), CHOSEN)

                def split_low(first, low_at):
                    for k in range(2):
                        for half in range(NH):
                            dve.wait_ge(xt_high, first + (NH * k + half + 1))
                            dve.tensor_tensor(low_x(k, half), turned_x(k, half), high_x(k, half), ALU.subtract).then_inc(xt_drained, 1)
                    for c in range(TOP):
                        dve.wait_ge(fc_high_done, low_at + (c + 1))
                        dve.tensor_tensor(fc_low[:, c, :, :], fc_raw[:, c, :, :], fc_high[:, c, :, :], ALU.subtract).then_inc(fc_low_done, 1)

                def work(batch, more):
                    p = batch.odd
                    dve.wait_ge(pj_in[p], batch.pair * PJ_LOADS + PJ_LOADS)
                    for c in range(TOP):
                        g = gates[:, bass.ds(batch.times(TOP, c), 1)]
                        dve.tensor_scalar(pj[:, p, c, :, :], pj[:, p, c, :, :], g, None, ALU.mult).then_inc(scaled, 1)
                    dve.tensor_scalar(bias_0[:, :], pjb[:, p, 0, :], gates[:, bass.ds(batch.times(TOP), 1)], None, ALU.mult).then_inc(bias_half, 1)
                    dve.wait_ge(bias_half, batch.times(1, 1))
                    dve.scalar_tensor_tensor(pj_bias[:, p, :], pjb[:, p, 1, :], gates[:, bass.ds(batch.times(TOP, 1), 1)],
                                             bias_0[:, :], ALU.mult, ALU.add).then_inc(bias_done, 1)
                    if more:
                        next_x1(batch.times(1, 1), batch.times(TT, TT), batch.times(1, 1))
                    for half in range(NH):
                        if half == NH - 1 and more:
                            split_low(batch.times(4, 4), batch.times(TOP, TOP))
                        for pair in range(2):
                            i = 2 * half + pair
                            if i == 0:
                                dve.wait_ge(x1_kept, batch.times(1, 1))
                            dve.wait_ge(z_filled, batch.times(4, i + 1))
                            rows = nrm[:, bass.ds(batch.times(TT, 2 * i), 2), :]
                            dve.tensor_tensor(rows, z_ps[:, i % 2, 0:2 * D].rearrange("p (t d) -> p t d", d=D), rows,
                                              ALU.add).then_inc(z_drained, 1)
                            dve.wait_ge(z_drained, batch.times(4, i + 3))
                            for t in range(2):
                                r = batch.times(TT, 2 * i + t)
                                dve.bn_stats(stats[:, bass.ds(r, 1), :].rearrange("p a s -> p (a s)"),
                                             nrm[:, bass.ds(r, 1), :].rearrange("p a d -> p (a d)")).then_inc(stats2_done, 1)

                def next_x1(number, first, kept):
                    if kept is not None:
                        dve.wait_ge(x1_kept, kept)
                    x = x1[:, :, :]
                    dve.tensor_tensor(x, nrm[:, bass.ds(first, TT), :], a_b[:, :].unsqueeze(1).to_broadcast([P, TT, D]),
                                      ALU.mult).then_inc(x1_half, 1)
                    dve.wait_ge(x1_half, number + 1)
                    dve.tensor_tensor(x, x, c_b[:, :].unsqueeze(1).to_broadcast([P, TT, D]), ALU.add).then_inc(x1_done, 1)

                next_x1(0, 0, None)
                dve.wait_ge(small_pe, 5)
                mark(dve.tensor_copy(gates[:, :], fc_ps[:, 3, 0:B * TOP]), GATES)
                split_low(0, 0)
                by_batch(dve, work)
                dve.wait_ge(stats2_done, ROWS)
                global_norm(1, 6, VARIANCE_2, VARIANCE_2 + 1)
                o = overall[:, 1, :]
                mark(dve.tensor_scalar(a_b[:, :], ln_b[:, 2, :], o[:, 4:5], None, ALU.mult))
                mark(dve.tensor_scalar(c_b[:, :], a_b[:, :], o[:, 5:6], None, ALU.mult), ADDEND)
                dve.wait_ge(finished, 2 * B)
                for i, b in enumerate(LAST_ORDER):
                    rows = slice(TT * b, TT * (b + 1))
                    dve.scalar_tensor_tensor(nrm[:, rows, :], nrm[:, rows, :], o[:, 4:5], hid[:, rows, :],
                                             ALU.mult, ALU.add).then_inc(final_1, 1)
                    if b in BY_DVE:
                        dve.wait_ge(final_1, i + 1)
                        dve.tensor_tensor(nrm[:, rows, :], nrm[:, rows, :], c_b[:, :].unsqueeze(1).to_broadcast([P, TT, D]),
                                          ALU.add).then_inc(final_3, 1)

            @block.tensor
            def _(pe):
                def transpose(out, in_, one):
                    return pe.matmul(out, in_, one, is_transpose=True, start=True, stop=True)

                pe.wait_ge(const_done, 2)

                def averages(norm, moments_at):
                    pe.wait_ge(small, moments_at)
                    pe.matmul(xt_ps[:, norm, 0:2], average[:, :], moments[:, norm, :], start=True, stop=True).then_inc(small_pe, 1)
                    pe.wait_ge(small, moments_at + 3)
                    pe.matmul(xt_ps[:, norm, 4:5], average[:, :], spread[:, norm, 1:2], start=True, stop=True).then_inc(small_pe, 1)

                averages(0, MOMENTS)
                for b in range(B):
                    for k in range(KT):
                        ins = pe.matmul(fc_ps[0:KD, 1, B * k + b:B * k + b + 1], y_sums[:, b, KD * k:KD * (k + 1)],
                                        average[:, 0:1], start=True, stop=True)
                ins.then_inc(small_pe, 1)
                pe.wait_ge(consts_in, 16 * 7)
                pe.wait_ge(small, XMEAN)
                for k in range(KT):
                    ins = pe.matmul(fc_ps[0:B, 2, 0:E], xmean[:, k, :], rw[:, k, :], start=k == 0, stop=k == KT - 1)
                ins.then_inc(small_pe, 1)
                pe.wait_ge(rows_in, 32)
                pe.matmul(fc_ps[:, 3, 0:B * TOP], one_row[:, :], best_row[:, :], start=True, stop=True).then_inc(small_pe, 1)

                def turn(x1_at, first):
                    pe.wait_ge(x1_done, x1_at)
                    for k, features in enumerate((slice(0, P), slice(P, D))):
                        for half in range(NH):
                            pe.wait_ge(xt_drained, first + (NH * k + half + 1))
                            if k > 0:
                                pe.sem_inc(passed_pe, 1)
                            for t in range(4):
                                ins = transpose(turned_x(k, half)[:, P * t:P * (t + 1)], x1[:, 4 * half + t, features], ident[:, :])
                            ins.then_inc(xt_filled, 1)

                def work(batch, more):
                    p = batch.odd
                    for half in range(NH):
                        if half == 0:
                            pe.wait_ge(xt_drained, batch.times(4, 6))
                            pe.wait_ge(fc_low_done, batch.times(TOP, TOP))
                        for i in range(HT):
                            pe.wait_ge(gelu_done, batch.times(NH * HT, HT * half + i + 1))
                            hidden = slice(P * (i % FT), P * (i % FT + 1))
                            products = ((fc_high, 0, 0, P), (fc_high, 0, 1, P), (fc_low, 0, 0, P),
                                        (fc_high, 1, 2, P), (fc_low, 1, 2, THIRD))
                            for n, (w, k, x, rows) in enumerate(products):
                                ins = pe.matmul(fc_ps[:, i % 4, :], w[0:rows, i // FT, k, hidden],
                                                x1T[0:rows, x, HALF * half:HALF * (half + 1)],
                                                start=n == 0, stop=n == len(products) - 1)
                            ins.then_inc(fc_filled, 1)
                        if half == NH - 1 and more:
                            turn(batch.times(1, 2), batch.times(4, 4))
                        pe.wait_ge(scaled, batch.times(TOP, TOP))
                        pe.wait_ge(gelu_done, batch.times(NH * HT, HT * (half + 1) + 4))
                        for pair in range(2):
                            pe.wait_ge(z_drained, batch.times(4, 2 * half + pair + 1))
                            for t in range(2):
                                c = 2 * pair + t
                                for i in range(HT):
                                    ins = pe.matmul(z_ps[:, pair, D * t:D * (t + 1)], act_h[:, i, P * c:P * (c + 1)],
                                                    pj[:, p, i // FT, i % FT, :], start=i == 0, stop=i == HT - 1)
                            ins.then_inc(z_filled, 1)

                pe.wait_ge(small, GATES)
                turn(1, 0)
                by_batch(pe, work)
                averages(1, MOMENTS_2)


INPUTS = ("tok", "table", "wqk", "wv", "wo", "wk2", "wq2", "wvT2", "w2", "r_w", "r_b", "fc_w", "fc_b", "pj_w", "pj_b", "ln", "ln_cols")


def layout(given):
    import numpy as np

    out = {}
    ids = np.asarray(given["x"])
    out["tok"] = np.ascontiguousarray(ids.reshape(B * TT, P).T)
    out["table"] = np.asarray(given["L0_tok_weight"])
    q, k, v, o = (np.asarray(given["L0_attn_" + n]).T for n in ("Wq", "Wk", "Wv", "Wo"))

    def by_group(w):
        return w.reshape(D, G, GROUP, DH).transpose(1, 0, 3, 2).reshape(G, D, GROUP * DH)

    both = np.concatenate([by_group(q), by_group(k)], axis=2)
    out["wqk"] = np.ascontiguousarray(both.reshape(G, KT, KD, P).transpose(2, 0, 1, 3))
    out["wv"] = np.ascontiguousarray(v.reshape(KT, KD, D).transpose(1, 0, 2))
    out["wo"] = np.zeros((P, G, D), o.dtype)
    for h in range(GROUP):
        out["wo"][32 * h:32 * h + DH] = o.reshape(G, GROUP, DH, D)[:, h].transpose(1, 0, 2)

    def tall(w, b):
        rows = np.zeros((KD + 1, KT, w.shape[1]), w.dtype)
        rows[:KD] = w.reshape(KT, KD, -1).transpose(1, 0, 2)
        rows[KD, 1] = b
        return rows

    w1, b1 = np.asarray(given["L0_ffn_W1_w"]), np.asarray(given["L0_ffn_W1_b"])
    out["wq2"] = tall(w1[:, :D], b1[:D])
    out["wk2"] = tall(w1[:, D:2 * D], b1[D:2 * D])
    out["wvT2"] = np.ascontiguousarray(np.concatenate([w1[:, 2 * D:], b1[None, 2 * D:]]).T.reshape(KT, KD, D + 1).transpose(1, 0, 2))
    w, b = np.asarray(given["L0_ffn_W2_w"]), np.asarray(given["L0_ffn_W2_b"])
    out["w2"] = np.zeros((P, 2, D), w.dtype)
    out["w2"][:, 0], out["w2"][:THIRD, 1], out["w2"][THIRD, 1] = w[:P], w[P:], b
    for name, key in (("r_w", "r_w"), ("r_b", "r_b"), ("fc_w", "fc_w"), ("fc_b", "fc_b"), ("pj_w", "proj_w"), ("pj_b", "proj_b")):
        out[name] = np.asarray(given["L0_ffn_" + key])
    out["fc_b"] = np.ascontiguousarray(out["fc_b"].reshape(E, FT, P).transpose(0, 2, 1))
    norms = [np.asarray(given["L0_ffn_" + n]) for n in ("ln1_w", "ln1_b", "ln2_w", "ln2_b")]
    out["ln"] = np.stack(norms)
    out["ln_cols"] = np.ascontiguousarray(np.stack(norms[:2]).reshape(2, KT, KD).transpose(2, 0, 1))
    return out


def kernel(**inputs):
    import numpy as np
    import concourse.bacc as bacc
    from concourse.bass_utils import run_bass_kernel_spmd

    nc = bacc.Bacc("TRN2", target_bir_lowering=False, num_devices=1)
    laid = layout(inputs)
    arrays, args = {}, []
    for name in INPUTS:
        a = np.ascontiguousarray(laid[name])
        arrays[f"in_{name}"] = a
        args.append(nc.dram_tensor(f"in_{name}", a.shape, mybir.dt.from_np(a.dtype), kind="ExternalInput").ap())
    args.append(nc.dram_tensor("out_rows", (B, N, D), mybir.dt.float32, kind="ExternalOutput").ap())
    build(nc, *args)
    done = run_bass_kernel_spmd(nc, [arrays], core_ids=[0])
    return done.results[0]["out_rows"]
```
